# Optimizing a Trainium2 kernel written in Bass

```python
import numpy as np
import jax
import jax.numpy as jnp

def _softmax(x, axis=-1):
    return jax.nn.softmax(x, axis=axis)

def _gelu(x):
    return jax.nn.gelu(x, approximate=True)

def _silu(x):
    return jax.nn.silu(x)

def _sigmoid(x):
    return jax.nn.sigmoid(x)

def _layernorm(x, axis=-1, eps=1e-05):
    m = jnp.mean(x, axis=axis, keepdims=True)
    v = jnp.var(x, axis=axis, keepdims=True)
    return (x - m) / jnp.sqrt(v + eps)

def _scatter_add(tgt, idx, src, axis=0):
    return tgt.at[idx].add(src)

def _segment_sum(src, seg, n):
    return jax.ops.segment_sum(src, seg, n)
kernel_name = 'mk_vit_tower_postln_d1_tok_img768_r4_e30c38'

def setup_inputs(seed: int=0):
    np.random.seed(seed)
    _w = jnp.asarray

    def _rec_inputs():
        import jax
        import jax.numpy as jnp
        _rk = jax.random.key(seed)
        x = -0.00016672 + 0.999947 * jax.random.normal(jax.random.fold_in(_rk, 1), (16, 3, 96, 96), jnp.float32)
        return x
    x = _rec_inputs()

    def _L0_tok_setup():
        import jax, jax.numpy as jnp
        import numpy as np
        IMAGE_SIZE = 96
        PATCH = 16
        EMBED = 192
        NUM_PATCHES = (IMAGE_SIZE // PATCH) ** 2
        PATCH_DIM = PATCH * PATCH * 3

        def _patchify(x, patch):
            b, c, h, w = x.shape
            nh, nw = (h // patch, w // patch)
            x = x.reshape(b, c, nh, patch, nw, patch)
            x = x.transpose(0, 2, 4, 1, 3, 5)
            return x.reshape(b, nh * nw, c * patch * patch)
        key = jax.random.key(seed)
        k1, k2, k3, k4, k5 = jax.random.split(key, 5)
        x = jax.random.normal(k1, (64, 3, IMAGE_SIZE, IMAGE_SIZE), dtype=jnp.float32)
        W_emb = jax.random.normal(k2, (PATCH_DIM, EMBED), dtype=jnp.float32) * 0.02
        b_emb = jnp.zeros((EMBED,), dtype=jnp.float32)
        pos_embedding = jax.random.normal(k3, (1, NUM_PATCHES + 1, EMBED), dtype=jnp.float32) * 0.02
        cls_token = jax.random.normal(k4, (1, 1, EMBED), dtype=jnp.float32) * 0.02
        return {'x': x, 'W_emb': W_emb, 'b_emb': b_emb, 'pos_embedding': pos_embedding, 'cls_token': cls_token}
    _L0_tok_all = _L0_tok_setup()
    _L0_tok_in = {k: v for k, v in _L0_tok_all.items() if k in ('W_emb', 'b_emb', 'pos_embedding', 'cls_token')}
    del _L0_tok_all

    def _L0_attn_setup():
        import jax, jax.numpy as jnp
        import numpy as np
        D_IN = 192
        N_HEADS = 12
        HEAD_DIM = 192 // N_HEADS
        B, S = (4, 512)
        key = jax.random.key(seed)
        ks = jax.random.split(key, 10)
        sc = 0.02
        x = jax.random.normal(ks[0], (B, S, D_IN), dtype=jnp.float32)
        Wq = jax.random.normal(ks[1], (N_HEADS, D_IN, HEAD_DIM), dtype=jnp.float32) * sc
        Wk = jax.random.normal(ks[2], (N_HEADS, D_IN, HEAD_DIM), dtype=jnp.float32) * sc
        Wv = jax.random.normal(ks[3], (N_HEADS, D_IN, HEAD_DIM), dtype=jnp.float32) * sc
        bq = jax.random.normal(ks[4], (N_HEADS, HEAD_DIM), dtype=jnp.float32) * sc
        bk = jax.random.normal(ks[5], (N_HEADS, HEAD_DIM), dtype=jnp.float32) * sc
        bv = jax.random.normal(ks[6], (N_HEADS, HEAD_DIM), dtype=jnp.float32) * sc
        Wo = jax.random.normal(ks[7], (N_HEADS * HEAD_DIM, N_HEADS * HEAD_DIM), dtype=jnp.float32) * sc
        bo = jax.random.normal(ks[8], (N_HEADS * HEAD_DIM,), dtype=jnp.float32) * sc
        return {'x': x, 'Wq': Wq, 'Wk': Wk, 'Wv': Wv, 'bq': bq, 'bk': bk, 'bv': bv, 'Wo': Wo, 'bo': bo}
    _L0_attn_all = _L0_attn_setup()
    _L0_attn_in = {k: v for k, v in _L0_attn_all.items() if k in ('Wq', 'Wk', 'Wv', 'bq', 'bk', 'bv', 'Wo', 'bo')}
    del _L0_attn_all

    def _L0_ffn_setup():
        import jax, jax.numpy as jnp
        import numpy as np
        ALPHA = 1.702
        LIMIT = 7.0
        TOP_K = 2
        B, S, H, E, I = (2, 256, 192, 8, 192)
        key = jax.random.key(seed)
        ks = jax.random.split(key, 7)
        scale = 0.02
        return {'hidden_states': jax.random.normal(ks[0], (B, S, H), dtype=jnp.float32), 'Wr': jax.random.normal(ks[1], (H, E), dtype=jnp.float32) * scale, 'br': jax.random.normal(ks[2], (E,), dtype=jnp.float32) * scale, 'Wgu': jax.random.normal(ks[3], (E, H, 2 * I), dtype=jnp.float32) * scale, 'bgu': jax.random.normal(ks[4], (E, 2 * I), dtype=jnp.float32) * scale, 'Wd': jax.random.normal(ks[5], (E, I, H), dtype=jnp.float32) * scale, 'bd': jax.random.normal(ks[6], (E, H), dtype=jnp.float32) * scale}
    _L0_ffn_all = _L0_ffn_setup()
    _L0_ffn_in = {k: v for k, v in _L0_ffn_all.items() if k in ('Wr', 'br', 'Wgu', 'bgu', 'Wd', 'bd')}
    del _L0_ffn_all
    return {'x': x, 'L0_tok_W_emb': _L0_tok_in['W_emb'], 'L0_tok_b_emb': _L0_tok_in['b_emb'], 'L0_tok_pos_embedding': _L0_tok_in['pos_embedding'], 'L0_tok_cls_token': _L0_tok_in['cls_token'], 'L0_attn_Wq': _L0_attn_in['Wq'], 'L0_attn_Wk': _L0_attn_in['Wk'], 'L0_attn_Wv': _L0_attn_in['Wv'], 'L0_attn_bq': _L0_attn_in['bq'], 'L0_attn_bk': _L0_attn_in['bk'], 'L0_attn_bv': _L0_attn_in['bv'], 'L0_attn_Wo': _L0_attn_in['Wo'], 'L0_attn_bo': _L0_attn_in['bo'], 'L0_ffn_Wr': _L0_ffn_in['Wr'], 'L0_ffn_br': _L0_ffn_in['br'], 'L0_ffn_Wgu': _L0_ffn_in['Wgu'], 'L0_ffn_bgu': _L0_ffn_in['bgu'], 'L0_ffn_Wd': _L0_ffn_in['Wd'], 'L0_ffn_bd': _L0_ffn_in['bd']}

def reference(x, L0_tok_W_emb, L0_tok_b_emb, L0_tok_pos_embedding, L0_tok_cls_token, L0_attn_Wq, L0_attn_Wk, L0_attn_Wv, L0_attn_bq, L0_attn_bk, L0_attn_bv, L0_attn_Wo, L0_attn_bo, L0_ffn_Wr, L0_ffn_br, L0_ffn_Wgu, L0_ffn_bgu, L0_ffn_Wd, L0_ffn_bd):
    import jax
    import jax.numpy as jnp

    def _L0_tok_ref(x, W_emb, b_emb, pos_embedding, cls_token):
        import jax, jax.numpy as jnp
        import numpy as np
        IMAGE_SIZE = 96
        PATCH = 16
        EMBED = 192
        NUM_PATCHES = (IMAGE_SIZE // PATCH) ** 2
        PATCH_DIM = PATCH * PATCH * 3

        def _patchify(x, patch):
            b, c, h, w = x.shape
            nh, nw = (h // patch, w // patch)
            x = x.reshape(b, c, nh, patch, nw, patch)
            x = x.transpose(0, 2, 4, 1, 3, 5)
            return x.reshape(b, nh * nw, c * patch * patch)
        b = x.shape[0]
        patches = _patchify(x, PATCH)
        tok = jnp.einsum('bnd,de->bne', patches, W_emb) + b_emb
        cls = jnp.broadcast_to(cls_token, (b, 1, EMBED))
        tok = jnp.concatenate([cls, tok], axis=1)
        return tok + pos_embedding[:, :tok.shape[1], :]

    def _L0_attn_ref(x, Wq, Wk, Wv, bq, bk, bv, Wo, bo):
        import jax, jax.numpy as jnp
        import numpy as np
        D_IN = 192
        N_HEADS = 12
        HEAD_DIM = 192 // N_HEADS
        B, S = (4, 512)
        b, n, _ = x.shape
        q = jnp.einsum('bnd,hdk->bhnk', x, Wq) + bq[None, :, None, :]
        k = jnp.einsum('bnd,hdk->bhnk', x, Wk) + bk[None, :, None, :]
        v = jnp.einsum('bnd,hdk->bhnk', x, Wv) + bv[None, :, None, :]
        scores = jnp.einsum('bhqk,bhsk->bhqs', q, k)
        causal = jnp.tril(jnp.ones((n, n), dtype=bool))
        scores = jnp.where(causal[None, None, :, :], scores, -jnp.inf)
        scale = 1.0 / jnp.sqrt(jnp.asarray(HEAD_DIM, dtype=scores.dtype))
        weights = jax.nn.softmax(scores * scale, axis=-1)
        ctx = jnp.einsum('bhqs,bhsk->bhqk', weights, v)
        ctx = ctx.transpose(0, 2, 1, 3).reshape(b, n, N_HEADS * HEAD_DIM)
        return ctx @ Wo + bo

    def _L0_ffn_ref(hidden_states, Wr, br, Wgu, bgu, Wd, bd):
        import jax, jax.numpy as jnp
        import numpy as np
        ALPHA = 1.702
        LIMIT = 7.0
        TOP_K = 2
        B, S, H, E, I = (2, 256, 192, 8, 192)
        logits = jnp.einsum('bsh,he->bse', hidden_states, Wr) + br
        topk_vals, topk_idx = jax.lax.top_k(logits, TOP_K)
        router_scores = jax.nn.softmax(topk_vals, axis=-1)
        gu = jnp.einsum('bsh,ehf->bsef', hidden_states, Wgu) + bgu
        gu = jnp.minimum(gu, LIMIT)
        gate = gu[..., :I]
        up = jnp.maximum(gu[..., I:], -LIMIT)
        glu = gate * jax.nn.sigmoid(gate * ALPHA)
        activated = (up + 1.0) * glu
        down = jnp.einsum('bsei,eih->bseh', activated, Wd) + bd
        sel = jnp.take_along_axis(down, topk_idx[..., None], axis=2)
        output = jnp.sum(sel * router_scores[..., None], axis=2)
        return output
    h = _L0_tok_ref(x, L0_tok_W_emb, L0_tok_b_emb, L0_tok_pos_embedding, L0_tok_cls_token)
    h = _layernorm(h + _L0_attn_ref(h, L0_attn_Wq, L0_attn_Wk, L0_attn_Wv, L0_attn_bq, L0_attn_bk, L0_attn_bv, L0_attn_Wo, L0_attn_bo), axis=-1)
    h = _layernorm(h + _L0_ffn_ref(h, L0_ffn_Wr, L0_ffn_br, L0_ffn_Wgu, L0_ffn_bgu, L0_ffn_Wd, L0_ffn_bd), axis=-1)
    return h

_drawn_inputs = setup_inputs


def setup_inputs(seed=0):
    import zlib

    import numpy as np

    out = dict(_drawn_inputs(seed))
    spreads = {'L0_tok_b_emb': (0.0, 0.1)}
    factors = {'L0_attn_Wq': 8.0,
     'L0_attn_Wk': 8.0,
     'L0_attn_bq': 64.0,
     'L0_attn_bk': 64.0,
     'L0_ffn_br': 8.0,
     'L0_ffn_bgu': 24.173,
     'L0_ffn_bd': 3.964}
    for name, (base, spread) in spreads.items():
        noise = np.random.default_rng([zlib.crc32(name.encode()), seed]).standard_normal(out[name].shape)
        drawn = base * np.exp(spread * noise) if base else spread * noise
        out[name] = jnp.asarray(drawn.astype(out[name].dtype))
    for name, factor in factors.items():
        out[name] = (out[name] * factor).astype(out[name].dtype)
    return out
```

```python
from contextlib import ExitStack

import concourse.bass as bass
from concourse import mybir

F32 = mybir.dt.float32
F32R = mybir.dt.float32r
BF16 = mybir.dt.bfloat16
U32 = mybir.dt.uint32
ALU = mybir.AluOpType
ACT = mybir.ActivationFunctionType
AX_X = mybir.AxisListType.X

P = 128
IMAGES, SEQ, D = 16, 37, 192
TOKENS = IMAGES * SEQ
HALF = TOKENS // 2
DB = D - P
PATCH_DIM = 768
CHUNKS = PATCH_DIM // P
HEADS, HD = 12, 16
PAIRS, MEMBERS = IMAGES // 2, 2
QG = 3
QH = HEADS // QG
VG = 4
VH = HEADS // VG
VW = 64
PAIR_TOKENS = MEMBERS * SEQ
SCORES = HEADS * SEQ
KEYS = VH * SEQ
EXPERTS, INNER = 8, 192
FT = EXPERTS * INNER // P
TILES = 5
PADDED = TILES * P
LAST = TOKENS - (TILES - 1) * P
PARTS = [(0, 2), (2, 5)]
X_RING = 2
GU = 4
ATT_SCALE = 0.25
ALPHA, LIMIT, EPS = 1.702, 7.0, 1e-5
MASKED = -1e37

_COLS = [("pos_a", SEQ), ("pos_b", SEQ), ("bemb_a", 1), ("bemb_b", 1), ("cls_a", 1), ("cls_b", 1),
         ("bq", QG), ("bk", QG), ("bv", 2), ("bg", FT), ("bu", FT), ("br", EXPERTS),
         ("wr_a", EXPERTS), ("wr_b", EXPERTS), ("head_mask", QH), ("value_mask", VH * HD),
         ("causal", SEQ), ("ident", P), ("bd", D)]
COL = {}
_at = 0
for _name, _n in _COLS:
    COL[_name] = (_at, _at + _n)
    _at += _n
SMALL = _at


def part_range(part):
    a, b = PARTS[part]
    return a * P, min(b * P, TOKENS) - a * P


def build_program(nc, x_t, w_emb, small, w_qk, w_v, w_o, sel, w_gu, w_d, out):
    with ExitStack() as ctx:
        def sb(stack, name, shape, dt=F32):
            return stack.enter_context(nc.sbuf_tensor(name, shape, dt))

        def sem(name):
            return ctx.enter_context(nc.semaphore(name))

        sm = sb(ctx, "sm", [P, SMALL])
        ident_bf = sb(ctx, "ident_bf", [P, P], BF16)
        causal_bf = sb(ctx, "causal_bf", [P, SEQ], BF16)
        bk_masked = sb(ctx, "bk_masked", [P, QG, QH])
        bu1 = sb(ctx, "bu1", [P, FT])
        eps = sb(ctx, "eps", [P, 1])
        expert_ids = sb(ctx, "expert_ids", [P, EXPERTS])
        wr_hi = sb(ctx, "wr_hi", [P, 2 * EXPERTS], F32R)
        wr_lo = sb(ctx, "wr_lo", [P, 2 * EXPERTS], F32R)
        bd_hi = sb(ctx, "bd_hi", [40, D], F32R)
        bd_lo = sb(ctx, "bd_lo", [40, D], F32R)
        res_a = sb(ctx, "res_a", [P, PADDED])
        res_b = sb(ctx, "res_b", [DB, PADDED])
        wo_sb = sb(ctx, "wo_sb", [P, 2, D])
        h1 = sb(ctx, "h1", [P, TILES, D])
        h1_ahi = sb(ctx, "h1_ahi", [P, PADDED], F32R)
        h1_alo = sb(ctx, "h1_alo", [P, PADDED], F32R)
        h1_bst = sb(ctx, "h1_bst", [P, PADDED], F32R)
        stats = sb(ctx, "stats", [P, TILES, 6])
        mv = sb(ctx, "mv", [P, TILES, 2])
        std = sb(ctx, "std", [P, TILES])
        rstd = sb(ctx, "rstd", [P, TILES])
        logits = sb(ctx, "logits", [P, TILES, EXPERTS])
        top = sb(ctx, "top", [P, TILES, EXPERTS])
        top_id = sb(ctx, "top_id", [P, TILES, EXPERTS], U32)
        top_idf = sb(ctx, "top_idf", [P, TILES, 2])
        gap = sb(ctx, "gap", [P, TILES])
        share = sb(ctx, "share", [P, 2, TILES])
        pick = sb(ctx, "pick", [P, 2, TILES, EXPERTS])
        route = sb(ctx, "route", [P, TILES, EXPERTS])
        route_st = sb(ctx, "route_st", [40, PADDED], F32R)
        sel_sb = sb(ctx, "sel_sb", [40, FT * P], F32R)
        stage = sb(ctx, "stage", [P, 2, FT * P])
        wd_hi = sb(ctx, "wd_hi", [P, FT, D], F32R)
        wd_lo = sb(ctx, "wd_lo", [P, FT, D], F32R)
        y2 = sb(ctx, "y2", [P, 2, D])
        result = sb(ctx, "result", [P, 2, D])
        warm = sb(ctx, "warm", [P, 1])

        with ExitStack() as early:
            x_hi = sb(early, "x_hi", [P, X_RING, TOKENS], F32R)
            x_lo = sb(early, "x_lo", [P, X_RING, TOKENS], F32R)
            x_raw = sb(early, "x_raw", [P, CHUNKS, TOKENS])
            we_raw = sb(early, "we_raw", [P, CHUNKS, D])
            we_hi = sb(early, "we_hi", [P, CHUNKS, D], F32R)
            we_lo = sb(early, "we_lo", [P, CHUNKS, D], F32R)
            sel_raw = sb(early, "sel_raw", [40, FT * P])
            wqk_raw = sb(early, "wqk_raw", [P, 2, 2, D])
            wv_raw = sb(early, "wv_raw", [P, 2, D])
        wgu_hi = sb(ctx, "wgu_hi", [P, GU, FT * P], F32R)
        wgu_lo = sb(ctx, "wgu_lo", [P, GU, FT * P], F32R)

        with ExitStack() as att:
            keys = sb(att, "keys", [P, QG, PAIRS, QH, SEQ])
            values = sb(att, "values", [KEYS, MEMBERS, PAIRS, VG, VW])
            ctx_t = sb(att, "ctx_t", [P, 2, PADDED])
            h_ahi = sb(att, "h_ahi", [P, TOKENS], F32R)
            h_alo = sb(att, "h_alo", [P, TOKENS], F32R)
            h_bst = sb(att, "h_bst", [P, TOKENS], F32R)
            queries = sb(att, "queries", [P, QG, PAIRS, PAIR_TOKENS])
            rep = [sb(att, f"rep_{n}", [P, IMAGES, VH, SEQ], F32R) for n in ("ahi", "alo", "bst")]
            wv_hi = sb(att, "wv_hi", [P, 2, D], F32R)
            wv_lo = sb(att, "wv_lo", [P, 2, D], F32R)
            with ExitStack() as proj:
                wqk_hi = sb(proj, "wqk_hi", [P, 2, 2, QG, 3 * DB], F32R)
                wqk_lo = sb(proj, "wqk_lo", [P, 2, 2, QG, 3 * DB], F32R)
            shifted = sb(att, "shifted", [PAIR_TOKENS, 2, SCORES])
            expd = sb(att, "expd", [PAIR_TOKENS, 2, SCORES])
            probs = sb(att, "probs", [PAIR_TOKENS, 2, SCORES])
            probs_t = sb(att, "probs_t", [KEYS, 2, VG, PAIR_TOKENS])
            top_score = sb(att, "top_score", [PAIR_TOKENS, 2, HEADS])
            prob_sum = sb(att, "prob_sum", [PAIR_TOKENS, 2, HEADS])
            prob_inv = sb(att, "prob_inv", [PAIR_TOKENS, 2, HEADS])
        NMAX = part_range(1)[1]
        RING = 3
        gate = sb(ctx, "gate", [P, RING, NMAX])
        up = sb(ctx, "up", [P, RING, NMAX])
        sig = sb(ctx, "sig", [P, RING, NMAX])
        spread = sb(ctx, "spread", [P, RING, NMAX])
        sig_w = sb(ctx, "sig_w", [P, RING, NMAX])
        glu = sb(ctx, "glu", [P, RING, NMAX])
        hid = sb(ctx, "hid", [P, RING, NMAX])
        hid_hi = sb(ctx, "hid_hi", [P, RING, NMAX], F32R)
        hid_lo = sb(ctx, "hid_lo", [P, RING, NMAX], F32R)

        bank = [ctx.enter_context(nc.psum_tensor(f"bank{i}", [P, 512], F32)) for i in range(8)]

        x_in = [sem(f"x_in{c}") for c in range(CHUNKS)]
        we_in, small_in, wqk_in, wv_in, wo_in, sel_in = (
            sem(n) for n in ("we_in", "small_in", "wqk_in", "wv_in", "wo_in", "sel_in"))
        stage_in = [sem(f"stage_in{i}") for i in range(6)]
        out_done = [sem(f"out_done{i}") for i in range(TILES)]
        pool_zero = sem("pool_zero")
        prep_done = sem("prep_done")
        x_hi_done, x_lo_done = sem("x_hi_done"), sem("x_lo_done")
        we_hi_done, we_lo_done = sem("we_hi_done"), sem("we_lo_done")
        emb_chunk, emb_done = sem("emb_chunk"), sem("emb_done")
        res_done, h_hi_done, h_lo_done = sem("res_done"), sem("h_hi_done"), sem("h_lo_done")
        wqk_hi_done, wqk_lo_done = sem("wqk_hi_done"), sem("wqk_lo_done")
        qk_ps, q_done, k_done = sem("qk_ps"), sem("q_done"), sem("k_done")
        rep_done, v_ps, v_done = sem("rep_done"), sem("v_ps"), sem("v_done")
        scores_ps, top_done, shift_done, exp_done = (
            sem(n) for n in ("scores_ps", "top_done", "shift_done", "exp_done"))
        sum_done, inv_done, probs_done = sem("sum_done"), sem("inv_done"), sem("probs_done")
        probs_ps, probs_t_done, ctx_ps, ctx_done = (
            sem(n) for n in ("probs_ps", "probs_t_done", "ctx_ps", "ctx_done"))
        y_ps, stats_done, mv_done, std_done, rstd_done, h1_done = (
            sem(n) for n in ("y_ps", "stats_done", "mv_done", "std_done", "rstd_done", "h1_done"))
        h1t_ps, h1_hi_done, h1_lo_done = sem("h1t_ps"), sem("h1_hi_done"), sem("h1_lo_done")
        logit_ps, router, share_done, route_done = (
            sem(n) for n in ("logit_ps", "router", "share_done", "route_done"))
        route_ps, route_hi_done, route_lo_done = (
            sem(n) for n in ("route_ps", "route_hi_done", "route_lo_done"))
        split_hi, split_done = sem("split_hi"), sem("split_done")
        wv_hi_done, wv_lo_done, sel_done = sem("wv_hi_done"), sem("wv_lo_done"), sem("sel_done")
        spread_ps, gate_ps, up_ps = sem("spread_ps"), sem("gate_ps"), sem("up_ps")
        spread_done, gate_done, up_done, sig_done = (
            sem(n) for n in ("spread_done", "gate_done", "up_done", "sig_done"))
        sigw_done, glu_done, hid_done = sem("sigw_done"), sem("glu_done"), sem("hid_done")
        hid_hi_done, hid_lo_done, down_ps = sem("hid_hi_done"), sem("hid_lo_done"), sem("down_ps")
        y2_done, stats2_done, mv2_done, std2_done, rstd2_done, result_done = (
            sem(n) for n in ("y2_done", "stats2_done", "mv2_done", "std2_done", "rstd2_done", "result_done"))

        def col(name, rows=P):
            a, b = COL[name]
            return sm[0:rows, a:b]

        units = [(part, t) for part in range(2) for t in range(FT)]
        UNITS = len(units)
        DOWN_LAG = 2

        def slots(t, half):
            return t.rearrange("d (m p k) -> d p m k", m=MEMBERS, p=PAIRS)[:, 4 * half:4 * half + 4]

        def by_pair(t):
            return t.rearrange("d (p m k) -> d p m k", p=PAIRS // 2, m=MEMBERS)

        STAGES = 6
        DOWN_COLS = FT // 2 * D

        block = ctx.enter_context(nc.Block())

        @block.sync
        def _(sp):
            for c in range(CHUNKS):
                sp.dma_start(x_raw[:, c, :], x_t[:, c, :]).then_inc(x_in[c], 16)
            sp.dma_start(wqk_raw[:], w_qk).then_inc(wqk_in, 16)
            for i in range(STAGES):
                if i >= 2:
                    sp.wait_ge(split_done, i - 1)
                if i < GU:
                    sp.dma_start(stage[:, i % 2, :], w_gu[:, i, :]).then_inc(stage_in[i], 16)
                else:
                    lot = w_d[:, (i - GU) * DOWN_COLS:(i - GU + 1) * DOWN_COLS]
                    sp.dma_start(stage[:, i % 2, 0:DOWN_COLS], lot).then_inc(stage_in[i], 16)
            for i in range(TILES):
                rows = LAST if i == TILES - 1 else P
                sp.wait_ge(result_done, i + 1)
                sp.dma_start(out[i * P:i * P + rows, :], result[0:rows, i % 2, :]).then_inc(out_done[i], 16)
            for i in range(TILES):
                sp.wait_ge(out_done[i], 16)

        @block.gpsimd
        def _(pool):
            pool.memset(wqk_hi[:].bitcast(F32), 0.0).then_inc(pool_zero, 1)
            pool.memset(wqk_lo[:].bitcast(F32), 0.0).then_inc(pool_zero, 1)
            pool.wait_ge(we_in, 16)
            for c in range(CHUNKS):
                pool.tensor_scalar(we_hi[:, c, :], we_raw[:, c, :], 1.0, 1.0, ALU.mult, ALU.mult)\
                    .then_inc(we_hi_done, 1)
                pool.wait_ge(we_hi_done, c + 1)
                pool.tensor_tensor(we_lo[:, c, :], we_raw[:, c, :], we_hi[:, c, :].bitcast(F32),
                                   ALU.subtract).then_inc(we_lo_done, 1)
            pool.wait_ge(wqk_in, 16)
            pool.wait_ge(pool_zero, 2)
            for w in range(2):
                for r in range(2):
                    dst = wqk_hi[:, w, r, :, DB:2 * DB]
                    src = wqk_raw[:, w, r, :].rearrange("p (g c) -> p g c", g=QG)
                    pool.tensor_scalar(dst, src, 1.0, 1.0, ALU.mult, ALU.mult).then_inc(wqk_hi_done, 1)
                    pool.wait_ge(wqk_hi_done, 2 * w + r + 1)
                    pool.tensor_tensor(wqk_lo[:, w, r, :, DB:2 * DB], src, dst.bitcast(F32),
                                       ALU.subtract).then_inc(wqk_lo_done, 1)
            pool.memset(queries[:], 0.0).then_inc(pool_zero, 1)
            srcs = (h_ahi, h_alo, h_bst)
            for i, (dst, src) in enumerate(zip(rep, srcs)):
                if i == 0:
                    pool.wait_ge(h_hi_done, 4)
                    pool.wait_ge(h_lo_done, 4)
                view = src[:].bitcast(F32).rearrange("d (s k) -> d s k", s=IMAGES)
                pool.tensor_scalar(dst[:], view.unsqueeze(2).broadcast_to([P, IMAGES, VH, SEQ]), 1.0, 1.0,
                                   ALU.mult, ALU.mult).then_inc(rep_done, 1)
            pool.memset(values[:, :, :, :, VH * HD:VW], 0.0).then_inc(pool_zero, 1)
            pool.memset(ctx_t[:, :, TOKENS:PADDED], 0.0).then_inc(pool_zero, 1)

            def split(i):
                n = FT * P if i < GU else DOWN_COLS
                src = stage[:, i % 2, 0:n]
                lots = slice((i - GU) * (FT // 2), (i - GU + 1) * (FT // 2))
                hi = wgu_hi[:, i, :] if i < GU else wd_hi[:, lots, :].rearrange("p t n -> p (t n)")
                lo = wgu_lo[:, i, :] if i < GU else wd_lo[:, lots, :].rearrange("p t n -> p (t n)")
                pool.wait_ge(stage_in[i], 16)
                if i == 0:
                    pool.wait_ge(emb_done, 4)
                    pool.wait_ge(wqk_lo_done, 4)
                    pool.wait_ge(wv_lo_done, 1)
                    pool.wait_ge(sel_done, 1)
                pool.tensor_scalar(hi, src, 1.0, 1.0, ALU.mult, ALU.mult).then_inc(split_hi, 1)
                pool.wait_ge(split_hi, i + 1)
                pool.tensor_tensor(lo, src, hi.bitcast(F32), ALU.subtract).then_inc(split_done, 1)

            split(0)
            for p in range(PAIRS):
                pool.wait_ge(exp_done, p + 1)
                pool.wait_ge(inv_done, p + 1)
                if p >= 2:
                    pool.wait_ge(probs_ps, p - 1)
                pool.tensor_tensor(
                    probs[:, p % 2, :].rearrange("q (h k) -> q h k", h=HEADS),
                    expd[:, p % 2, :].rearrange("q (h k) -> q h k", h=HEADS),
                    prob_inv[:, p % 2, :].unsqueeze(2).broadcast_to([PAIR_TOKENS, HEADS, SEQ]),
                    ALU.mult).then_inc(probs_done, 1)
                if p % 2 == 0 and 1 + p // 2 < STAGES:
                    split(1 + p // 2)
            split(5)
            for u, (part, t) in enumerate(units):
                n = part_range(part)[1]
                r = u % RING
                pool.wait_ge(sig_done, u + 1)
                pool.wait_ge(spread_done, u + 1)
                pool.tensor_tensor(sig_w[:, r, 0:n], sig[:, r, 0:n], spread[:, r, 0:n], ALU.mult)\
                    .then_inc(sigw_done, 1)
                pool.wait_ge(sigw_done, u + 1)
                if u >= RING:
                    pool.wait_ge(hid_done, u - RING + 1)
                pool.tensor_tensor(glu[:, r, 0:n], sig_w[:, r, 0:n], gate[:, r, 0:n], ALU.mult)\
                    .then_inc(glu_done, 1)

        @block.scalar
        def _(act):
            act.dma_start(we_raw[:], w_emb).then_inc(we_in, 16)
            act.dma_start(sm[:], small).then_inc(small_in, 16)
            act.dma_start(wv_raw[:], w_v).then_inc(wv_in, 16)
            act.dma_start(wo_sb[:], w_o).then_inc(wo_in, 16)
            act.dma_start(sel_raw[:], sel).then_inc(sel_in, 16)
            for c in range(CHUNKS):
                act.wait_ge(x_in[c], 16)
                if c >= X_RING:
                    act.wait_ge(emb_chunk, c - X_RING + 1)
                act.activation(x_hi[:, c % X_RING, :], x_raw[:, c, :], ACT.Copy).then_inc(x_hi_done, 1)
            act.wait_ge(wv_in, 16)
            act.activation(wv_hi[:], wv_raw[:], ACT.Copy).then_inc(wv_hi_done, 1)
            for half in range(2):
                cols = slice(half * HALF, (half + 1) * HALF)
                act.wait_ge(res_done, 2 * half + 1)
                act.activation(slots(h_ahi[:], half), by_pair(res_a[:, cols]), ACT.Copy).then_inc(h_hi_done, 1)
                act.wait_ge(res_done, 2 * half + 2)
                act.activation(slots(h_bst[0:DB, :], half), by_pair(res_b[:, cols]), ACT.Copy)\
                    .then_inc(h_hi_done, 1)
            act.wait_ge(pool_zero, 3)
            for g in range(QG):
                act.wait_ge(qk_ps, 2 * g + 1)
                src = bank[4 + (2 * g) % 4][:, 0:HALF].rearrange("d (p k) -> d p k", p=PAIRS)
                for m in range(MEMBERS):
                    rows = slice(m * DB, (m + 1) * DB)
                    act.activation(queries[rows, g, :, m * SEQ:(m + 1) * SEQ], src[rows], ACT.Identity,
                                   bias=sm[rows, COL["bq"][0] + g:COL["bq"][0] + g + 1]).then_inc(q_done, 1)
            act.wait_ge(sel_in, 16)
            act.activation(sel_sb[:], sel_raw[:], ACT.Copy).then_inc(sel_done, 1)
            for p in range(PAIRS + 1):
                if p < PAIRS:
                    act.wait_ge(shift_done, p + 1)
                    if p >= 2:
                        act.wait_ge(probs_done, p - 1)
                    act.activation(expd[:, p % 2, :], shifted[:, p % 2, :], ACT.Exp, scale=ATT_SCALE)\
                        .then_inc(exp_done, 1)
                if p >= 1:
                    q = p - 1
                    act.wait_ge(probs_ps, q + 1)
                    if q >= 2:
                        act.wait_ge(ctx_ps, q - 1)
                    act.activation(probs_t[:, q % 2].rearrange("k g q -> k (g q)"),
                                   bank[q % 2][0:KEYS, 0:VG * PAIR_TOKENS], ACT.Copy)\
                        .then_inc(probs_t_done, 1)
            for i in range(TILES):
                act.wait_ge(mv_done, i + 1)
                act.activation(std[:, i:i + 1], mv[:, i, 1:2], ACT.Sqrt, bias=eps[:]).then_inc(std_done, 1)
            for part in range(2):
                c0 = PARTS[part][0] * P
                n = (PARTS[part][1] - PARTS[part][0]) * P
                act.wait_ge(h1t_ps, 2 * part + 1)
                act.activation(h1_ahi[:, c0:c0 + n], bank[2 * part][:, 0:n], ACT.Copy).then_inc(h1_hi_done, 1)
                act.wait_ge(h1t_ps, 2 * part + 2)
                act.activation(h1_bst[0:DB, c0:c0 + n], bank[2 * part + 1][0:DB, 0:n], ACT.Copy)\
                    .then_inc(h1_hi_done, 1)
            for part in range(2):
                a, b = PARTS[part]
                act.wait_ge(router, 5 * part + 4)
                for k, sign in ((0, 1.0), (1, -1.0)):
                    act.activation(share[:, k, a:b], gap[:, a:b], ACT.Sigmoid, scale=sign).then_inc(share_done, 1)
            for part in range(2):
                a, b = PARTS[part]
                act.wait_ge(route_ps, part + 1)
                act.activation(route_st[0:EXPERTS, a * P:b * P], bank[(7, 5)[part]][0:EXPERTS, 0:(b - a) * P],
                               ACT.Copy).then_inc(route_hi_done, 1)

            def hidden_hi(u):
                n = part_range(units[u][0])[1]
                r = u % RING
                act.wait_ge(hid_done, u + 1)
                if u >= RING:
                    act.wait_ge(down_ps, u - RING + 1)
                act.activation(hid_hi[:, r, 0:n], hid[:, r, 0:n], ACT.Copy).then_inc(hid_hi_done, 1)

            for u, (part, t) in enumerate(units):
                n = part_range(part)[1]
                r = u % RING
                act.wait_ge(spread_ps, u + 1)
                if u >= RING:
                    act.wait_ge(sigw_done, u - RING + 1)
                act.activation(spread[:, r, 0:n], bank[6][:, 0:n], ACT.Copy).then_inc(spread_done, 1)
                act.wait_ge(gate_done, u + 1)
                act.activation(sig[:, r, 0:n], gate[:, r, 0:n], ACT.Sigmoid, scale=ALPHA).then_inc(sig_done, 1)
                if u >= 1:
                    hidden_hi(u - 1)
            hidden_hi(UNITS - 1)
            for i in range(TILES):
                rows = LAST if i == TILES - 1 else P
                act.wait_ge(mv2_done, i + 1)
                act.activation(std[0:rows, i:i + 1], mv[0:rows, i, 1:2], ACT.Sqrt, bias=eps[0:rows, :])\
                    .then_inc(std2_done, 1)

        @block.vector
        def _(dve):
            dve.memset(eps[:], EPS).then_inc(prep_done, 1)
            dve.memset(route_st[:].bitcast(F32), 0.0).then_inc(prep_done, 1)
            dve.memset(res_a[:, TOKENS:PADDED], 0.0).then_inc(prep_done, 1)
            dve.memset(res_b[:, TOKENS:PADDED], 0.0).then_inc(prep_done, 1)
            for e in range(EXPERTS):
                dve.memset(expert_ids[:, e:e + 1], float(e)).then_inc(prep_done, 1)
            dve.wait_ge(small_in, 16)
            for part, rows in (("a", P), ("b", DB)):
                pos, bias, cls = (col(f"{n}_{part}", rows) for n in ("pos", "bemb", "cls"))
                dve.tensor_scalar(pos[:, 1:SEQ], pos[:, 1:SEQ], bias, None, ALU.add).then_inc(prep_done, 1)
                dve.tensor_scalar(pos[:, 0:1], pos[:, 0:1], cls, None, ALU.add).then_inc(prep_done, 1)
            dve.tensor_copy(ident_bf[:], col("ident")).then_inc(prep_done, 1)
            dve.tensor_copy(causal_bf[:], col("causal")).then_inc(prep_done, 1)
            dve.tensor_tensor(bk_masked[:], col("bk").unsqueeze(2).broadcast_to([P, QG, QH]),
                              col("head_mask").unsqueeze(1).broadcast_to([P, QG, QH]), ALU.mult)\
                .then_inc(prep_done, 1)
            dve.tensor_scalar(bu1[:], col("bu"), 1.0, None, ALU.add).then_inc(prep_done, 1)
            wr = sm[:, COL["wr_a"][0]:COL["wr_b"][1]]
            dve.tensor_copy(wr_hi[:], wr).then_inc(prep_done, 1)
            dve.tensor_copy(bd_hi[:], col("bd", 40)).then_inc(prep_done, 1)
            PREP = 22
            dve.wait_ge(prep_done, PREP)
            dve.tensor_tensor(wr_lo[:], wr, wr_hi[:].bitcast(F32), ALU.subtract).then_inc(prep_done, 1)
            dve.tensor_tensor(bd_lo[:], col("bd", 40), bd_hi[:].bitcast(F32), ALU.subtract)\
                .then_inc(prep_done, 1)
            for c in range(CHUNKS):
                dve.wait_ge(x_hi_done, c + 1)
                if c >= X_RING:
                    dve.wait_ge(emb_chunk, c - X_RING + 1)
                dve.tensor_tensor(x_lo[:, c % X_RING, :], x_raw[:, c, :], x_hi[:, c % X_RING, :].bitcast(F32),
                                  ALU.subtract).then_inc(x_lo_done, 1)
            dve.wait_ge(wv_hi_done, 1)
            dve.tensor_tensor(wv_lo[:], wv_raw[:], wv_hi[:].bitcast(F32), ALU.subtract)\
                .then_inc(wv_lo_done, 1)
            for half in range(2):
                cols = slice(half * HALF, (half + 1) * HALF)
                for r, (res, rows, part) in enumerate(((res_a, P, "a"), (res_b, DB, "b"))):
                    dve.wait_ge(emb_done, 2 * half + r + 1)
                    dve.tensor_tensor(
                        res[:, cols].rearrange("d (b k) -> d b k", k=SEQ),
                        bank[2 * r + half][0:rows, 0:HALF].rearrange("d (b k) -> d b k", k=SEQ),
                        col(f"pos_{part}", rows).unsqueeze(1).broadcast_to([rows, IMAGES // 2, SEQ]),
                        ALU.add).then_inc(res_done, 1)
            for half in range(2):
                cols = slice(half * HALF, (half + 1) * HALF)
                dve.wait_ge(res_done, 2 * half + 2)
                dve.wait_ge(h_hi_done, 2 * half + 1)
                dve.tensor_tensor(slots(h_alo[:], half), by_pair(res_a[:, cols]),
                                  slots(h_ahi[:].bitcast(F32), half), ALU.subtract).then_inc(h_lo_done, 1)
                dve.wait_ge(h_hi_done, 2 * half + 2)
                dve.tensor_tensor(slots(h_bst[DB:P, :], half), by_pair(res_b[:, cols]),
                                  slots(h_bst[0:DB, :].bitcast(F32), half), ALU.subtract)\
                    .then_inc(h_lo_done, 1)
            for g in range(QG):
                dve.wait_ge(qk_ps, 2 * g + 2)
                src = bank[4 + (2 * g + 1) % 4][:, 0:HALF].rearrange("d (p k) -> d p k", p=PAIRS)
                bk = sm[:, COL["bk"][0] + g:COL["bk"][0] + g + 1]
                for h in range(QH):
                    keep = sm[:, COL["head_mask"][0] + h:COL["head_mask"][0] + h + 1]
                    dve.tensor_scalar(keys[:, g, :, h, :], src, bk, keep, ALU.add, ALU.mult).then_inc(k_done, 1)

            def value_rows(p):
                dve.wait_ge(v_ps, p + 1)
                if p == 0:
                    dve.wait_ge(pool_zero, 4)
                src = bank[4 + p % 2][0:KEYS, 0:MEMBERS * D].rearrange("k (s c) -> k s c", c=VH * HD)
                keep = col("value_mask", KEYS).unsqueeze(1).broadcast_to([KEYS, MEMBERS * VG, VH * HD])
                dst = values[:, :, p, :, 0:VH * HD]
                dve.tensor_tensor(dst, src.rearrange("k (m g) c -> k m g c", m=MEMBERS),
                                  keep.rearrange("k (m g) c -> k m g c", m=MEMBERS), ALU.mult)\
                    .then_inc(v_done, 1)

            def by_head(t):
                return t.rearrange("q (h k) -> q h k", h=HEADS)

            def shift(p):
                dve.wait_ge(scores_ps, p + 1)
                src = by_head(bank[6 + p % 2][0:PAIR_TOKENS, 0:SCORES])
                dve.tensor_reduce(top_score[:, p % 2, :], src, AX_X, ALU.max).then_inc(top_done, 1)
                dve.wait_ge(top_done, p + 1)
                if p >= 2:
                    dve.wait_ge(exp_done, p - 1)
                dve.tensor_tensor(by_head(shifted[:, p % 2, :]), src,
                                  top_score[:, p % 2, :].unsqueeze(2).broadcast_to([PAIR_TOKENS, HEADS, SEQ]),
                                  ALU.subtract).then_inc(shift_done, 1)

            def sums(p):
                dve.wait_ge(exp_done, p + 1)
                dve.tensor_reduce(prob_sum[:, p % 2, :], by_head(expd[:, p % 2, :]), AX_X, ALU.add)\
                    .then_inc(sum_done, 1)
                dve.wait_ge(sum_done, p + 1)
                if p >= 2:
                    dve.wait_ge(probs_done, p - 1)
                dve.reciprocal(prob_inv[:, p % 2, :], prob_sum[:, p % 2, :]).then_inc(inv_done, 1)

            def context(p):
                dve.wait_ge(ctx_ps, p + 1)
                dve.tensor_tensor(
                    ctx_t[:, :, p * PAIR_TOKENS:(p + 1) * PAIR_TOKENS],
                    bank[2 + p % 2][:, 0:2 * PAIR_TOKENS].rearrange("d (c q) -> d c q", c=2),
                    col("bv").unsqueeze(2).broadcast_to([P, 2, PAIR_TOKENS]), ALU.add).then_inc(ctx_done, 1)

            for p in range(PAIRS + 2):
                if p < PAIRS:
                    shift(p)
                    value_rows(p)
                if 1 <= p <= PAIRS:
                    sums(p - 1)
                if p >= 2:
                    context(p - 2)
            for i in range(TILES + 1):
                if i < TILES:
                    y = bank[4 + i % 2][:, 0:D]
                    dve.wait_ge(y_ps, i + 1)
                    dve.bn_stats(stats[:, i, :], y).then_inc(stats_done, 1)
                    dve.wait_ge(stats_done, i + 1)
                    dve.bn_aggr(mv[:, i, :], stats[:, i, :]).then_inc(mv_done, 1)
                if i >= 1:
                    j = i - 1
                    dve.wait_ge(std_done, j + 1)
                    dve.reciprocal(rstd[:, j:j + 1], std[:, j:j + 1]).then_inc(rstd_done, 1)
                    dve.wait_ge(rstd_done, j + 1)
                    dve.wait_ge(mv_done, j + 1)
                    dve.tensor_scalar(h1[:, j, :], bank[4 + j % 2][:, 0:D], mv[:, j, 0:1], rstd[:, j:j + 1],
                                      ALU.subtract, ALU.mult).then_inc(h1_done, 1)
            for part in range(2):
                c0 = PARTS[part][0] * P
                n = (PARTS[part][1] - PARTS[part][0]) * P
                dve.wait_ge(h1_hi_done, 2 * part + 1)
                dve.tensor_tensor(h1_alo[:, c0:c0 + n], bank[2 * part][:, 0:n],
                                  h1_ahi[:, c0:c0 + n].bitcast(F32), ALU.subtract).then_inc(h1_lo_done, 1)
                dve.wait_ge(h1_hi_done, 2 * part + 2)
                dve.tensor_tensor(h1_bst[DB:P, c0:c0 + n], bank[2 * part + 1][0:DB, 0:n],
                                  h1_bst[0:DB, c0:c0 + n].bitcast(F32), ALU.subtract).then_inc(h1_lo_done, 1)
            for part in range(2):
                a, b = PARTS[part]
                n = b - a
                r0 = 5 * part
                dve.wait_ge(logit_ps, part + 1)
                dve.tensor_tensor(logits[:, a:b, :],
                                  bank[(6, 4)[part]][:, 0:n * EXPERTS].rearrange("t (i e) -> t i e", e=EXPERTS),
                                  col("br").unsqueeze(1).broadcast_to([P, n, EXPERTS]), ALU.add)\
                    .then_inc(router, 1)
                dve.wait_ge(router, r0 + 1)
                for i in range(a, b):
                    ins = dve.max(top[:, i, :], logits[:, i, :])
                ins.then_inc(router, 1)
                dve.wait_ge(router, r0 + 2)
                for i in range(a, b):
                    ins = dve.max_index(top_id[:, i, :], top[:, i, :], logits[:, i, :])
                ins.then_inc(router, 1)
                dve.tensor_tensor(gap[:, a:b], top[:, a:b, 0], top[:, a:b, 1], ALU.subtract).then_inc(router, 1)
                dve.wait_ge(router, r0 + 4)
                dve.tensor_copy(top_idf[:, a:b, :], top_id[:, a:b, 0:2]).then_inc(router, 1)
                dve.wait_ge(router, r0 + 5)
                for k in range(2):
                    ins = dve.tensor_tensor(pick[:, k, a:b, :],
                                            expert_ids[:].unsqueeze(1).broadcast_to([P, n, EXPERTS]),
                                            top_idf[:, a:b, k:k + 1].broadcast_to([P, n, EXPERTS]), ALU.is_equal)
                ins.then_inc(route_done, 1)
                dve.wait_ge(route_done, 3 * part + 1)
                dve.wait_ge(share_done, 2 * part + 2)
                for k in range(2):
                    ins = dve.tensor_tensor(pick[:, k, a:b, :], pick[:, k, a:b, :],
                                            share[:, k, a:b].unsqueeze(2).broadcast_to([P, n, EXPERTS]),
                                            ALU.mult)
                ins.then_inc(route_done, 1)
                dve.wait_ge(route_done, 3 * part + 2)
                dve.tensor_tensor(route[:, a:b, :], pick[:, 0, a:b, :], pick[:, 1, a:b, :], ALU.add)\
                    .then_inc(route_done, 1)
            for part in range(2):
                a, b = PARTS[part]
                dve.wait_ge(route_hi_done, part + 1)
                dve.tensor_tensor(route_st[32:40, a * P:b * P], bank[(7, 5)[part]][0:EXPERTS, 0:(b - a) * P],
                                  route_st[0:EXPERTS, a * P:b * P].bitcast(F32), ALU.subtract)\
                    .then_inc(route_lo_done, 1)

            def hidden(u):
                n = part_range(units[u][0])[1]
                r = u % RING
                dve.wait_ge(glu_done, u + 1)
                dve.wait_ge(up_done, u + 1)
                if u >= RING:
                    dve.wait_ge(hid_hi_done, u - RING + 1)
                    dve.wait_ge(hid_lo_done, u - RING + 1)
                dve.scalar_tensor_tensor(out=hid[:, r, 0:n], in0=up[:, r, 0:n], scalar=1.0 - LIMIT,
                                         in1=glu[:, r, 0:n], op0=ALU.max, op1=ALU.mult).then_inc(hid_done, 1)

            def hidden_lo(u):
                n = part_range(units[u][0])[1]
                r = u % RING
                dve.wait_ge(hid_hi_done, u + 1)
                if u >= RING:
                    dve.wait_ge(down_ps, u - RING + 1)
                dve.tensor_tensor(hid_lo[:, r, 0:n], hid[:, r, 0:n], hid_hi[:, r, 0:n].bitcast(F32),
                                  ALU.subtract).then_inc(hid_lo_done, 1)

            for u in range(UNITS + 2):
                if u < UNITS:
                    part, t = units[u]
                    n = part_range(part)[1]
                    r = u % RING
                    dve.wait_ge(gate_ps, u + 1)
                    if u >= RING:
                        dve.wait_ge(glu_done, u - RING + 1)
                    dve.tensor_scalar(gate[:, r, 0:n], bank[u % 2][:, 0:n],
                                      sm[:, COL["bg"][0] + t:COL["bg"][0] + t + 1], LIMIT, ALU.add, ALU.min)\
                        .then_inc(gate_done, 1)
                    dve.wait_ge(up_ps, u + 1)
                    if u >= RING:
                        dve.wait_ge(hid_done, u - RING + 1)
                    dve.tensor_scalar(up[:, r, 0:n], bank[2 + u % 2][:, 0:n], bu1[:, t:t + 1], LIMIT + 1.0,
                                      ALU.add, ALU.min).then_inc(up_done, 1)
                if 1 <= u <= UNITS:
                    hidden(u - 1)
                if u >= 2:
                    hidden_lo(u - 2)
            for i in range(TILES):
                rows = LAST if i == TILES - 1 else P
                acc = bank[7][0:rows, i * D:(i + 1) * D] if i < 2 else \
                    bank[4 + (i - 2) // 2][0:rows, (i % 2) * D:(i % 2 + 1) * D]
                dve.wait_ge(down_ps, FT if i < 2 else UNITS)
                y = y2[0:rows, i % 2, :]
                if i >= 2:
                    dve.wait_ge(result_done, i - 1)
                dve.tensor_tensor(y, acc, h1[0:rows, i, :], ALU.add).then_inc(y2_done, 1)
                dve.wait_ge(y2_done, i + 1)
                dve.bn_stats(stats[0:rows, i, :], y).then_inc(stats2_done, 1)
                dve.wait_ge(stats2_done, i + 1)
                dve.bn_aggr(mv[0:rows, i, :], stats[0:rows, i, :]).then_inc(mv2_done, 1)
                dve.wait_ge(std2_done, i + 1)
                dve.reciprocal(rstd[0:rows, i:i + 1], std[0:rows, i:i + 1]).then_inc(rstd2_done, 1)
                dve.wait_ge(rstd2_done, i + 1)
                dve.wait_ge(mv2_done, i + 1)
                if i >= 2:
                    dve.wait_ge(out_done[i - 2], 16)
                dve.tensor_scalar(result[0:rows, i % 2, :], y, mv[0:rows, i, 0:1], rstd[0:rows, i:i + 1],
                                  ALU.subtract, ALU.mult).then_inc(result_done, 1)

        @block.tensor
        def _(pe):
            outs = [(0, 0, P, 0), (2, P, D, 0), (1, 0, P, 1), (3, P, D, 1)]
            for c in range(CHUNKS):
                pe.wait_ge(we_lo_done, c + 1)
                terms = ((we_hi, x_hi, x_hi_done), (we_lo, x_hi, x_hi_done), (we_hi, x_lo, x_lo_done))
                for k, (w, x, ready) in enumerate(terms):
                    pe.wait_ge(ready, c + 1)
                    for b, d0, d1, half in outs:
                        mm = pe.matmul(bank[b][0:d1 - d0, 0:HALF], w[:, c, d0:d1],
                                       x[:, c % X_RING, half * HALF:(half + 1) * HALF],
                                       start=(c == 0 and k == 0), stop=(c == CHUNKS - 1 and k == 2))
                        if c == CHUNKS - 1 and k == 2:
                            mm.then_inc(emb_done, 1)
                if c < CHUNKS - 1:
                    mm.then_inc(emb_chunk, 1)

            pe.wait_ge(wqk_lo_done, 4)
            pe.wait_ge(h_lo_done, 4)
            for n in range(2 * QG):
                g, w = n // 2, n % 2
                ps = bank[4 + n % 4][:, 0:HALF]
                if n == 4:
                    pe.wait_ge(q_done, 2)
                if n == 5:
                    pe.wait_ge(k_done, QH)
                mms = 0
                for m in range(MEMBERS):
                    wc = slice(DB - m * DB, DB - m * DB + P)
                    hc = slice(m * HALF, (m + 1) * HALF)
                    for wt, r, h in ((wqk_hi, 0, h_ahi), (wqk_lo, 0, h_ahi), (wqk_hi, 0, h_alo),
                                     (wqk_hi, 1, h_bst), (wqk_lo, 1, h_bst)):
                        mm = pe.matmul(ps, wt[:, w, r, g, wc], h[:, hc], start=(mms == 0), stop=(mms == 9))
                        mms += 1
                mm.then_inc(qk_ps, 1)

            def scores(p):
                ps = bank[6 + p % 2]
                if p == 0:
                    pe.wait_ge(prep_done, 24)
                    pe.wait_ge(q_done, 2 * QG)
                    pe.wait_ge(k_done, QG * QH)
                if p >= 2:
                    pe.wait_ge(shift_done, p - 1)
                pe.matmul(ps[0:PAIR_TOKENS, 0:SCORES].rearrange("q (h k) -> q h k", h=HEADS),
                          ident_bf[0:PAIR_TOKENS, 0:PAIR_TOKENS],
                          causal_bf[0:PAIR_TOKENS, :].unsqueeze(1).broadcast_to([PAIR_TOKENS, HEADS, SEQ]),
                          start=True, stop=False)
                for g in range(QG):
                    mm = pe.matmul(ps[0:PAIR_TOKENS, g * QH * SEQ:(g + 1) * QH * SEQ], queries[:, g, p, :],
                                   keys[:, g, p].rearrange("d h k -> d (h k)"), start=False, stop=(g == QG - 1))
                mm.then_inc(scores_ps, 1)

            def pair_values(p):
                if p == 0:
                    pe.wait_ge(rep_done, 3)
                    pe.wait_ge(wv_lo_done, 1)
                if p >= 2:
                    pe.wait_ge(v_done, p - 1)
                for m in range(MEMBERS):
                    terms = ((rep[0], wv_hi, 0), (rep[0], wv_lo, 0), (rep[1], wv_hi, 0),
                             (rep[2], wv_hi, 1), (rep[2], wv_lo, 1))
                    for k, (h, wt, r) in enumerate(terms):
                        mm = pe.matmul(bank[4 + p % 2][0:KEYS, m * D:(m + 1) * D],
                                       h[:, m * PAIRS + p].rearrange("d v k -> d (v k)"), wt[:, r, :],
                                       start=(k == 0), stop=(k == 4))
                mm.then_inc(v_ps, 1)

            def turn(p):
                pe.wait_ge(probs_done, p + 1)
                if p >= 2:
                    pe.wait_ge(probs_t_done, p - 1)
                for g in range(VG):
                    mm = pe.transpose(bank[p % 2][0:KEYS, g * PAIR_TOKENS:(g + 1) * PAIR_TOKENS],
                                      probs[:, p % 2, g * KEYS:(g + 1) * KEYS],
                                      sm[0:PAIR_TOKENS, COL["ident"][0]:COL["ident"][0] + PAIR_TOKENS])
                mm.then_inc(probs_ps, 1)

            def contexts(p):
                pe.wait_ge(probs_t_done, p + 1)
                pe.wait_ge(v_done, p + 1)
                if p >= 2:
                    pe.wait_ge(ctx_done, p - 1)
                for m in range(MEMBERS):
                    for g in range(VG):
                        r0, c0 = VW * (g % 2), (g // 2) * PAIR_TOKENS + m * SEQ
                        mm = pe.matmul(bank[2 + p % 2][r0:r0 + VW, c0:c0 + SEQ], values[:, m, p, g, :],
                                       probs_t[:, p % 2, g, m * SEQ:(m + 1) * SEQ], start=True, stop=True)
                mm.then_inc(ctx_ps, 1)

            for p in range(PAIRS + 2):
                if p < PAIRS:
                    scores(p)
                    pair_values(p)
                if 1 <= p <= PAIRS:
                    turn(p - 1)
                if p >= 2:
                    contexts(p - 2)

            pe.wait_ge(wo_in, 16)
            ident = col("ident")
            for i in range(TILES):
                cols = slice(i * P, (i + 1) * P)
                y = bank[4 + i % 2]
                pe.wait_ge(ctx_done, min(PAIRS, -(-(i + 1) * P // PAIR_TOKENS)))
                if i < 2:
                    pe.wait_ge(v_done, PAIRS)
                else:
                    pe.wait_ge(h1_done, i - 1)
                pe.matmul(y[:, 0:D], ctx_t[:, 0, cols], wo_sb[:, 0, :], start=True, stop=False)
                pe.matmul(y[:, 0:D], ctx_t[:, 1, cols], wo_sb[:, 1, :], start=False, stop=False)
                pe.matmul(y[:, 0:P], res_a[:, cols], ident, start=False, stop=False)
                pe.matmul(y[:, P:D], res_b[:, cols], ident[0:DB, 0:DB], start=False, stop=True)\
                    .then_inc(y_ps, 1)
            for part in range(2):
                a, b = PARTS[part]
                for r, (c0, c1) in enumerate(((0, P), (P, D))):
                    for i in range(a, b):
                        pe.wait_ge(h1_done, i + 1)
                        mm = pe.transpose(bank[2 * part + r][0:c1 - c0, (i - a) * P:(i - a + 1) * P],
                                          h1[:, i, c0:c1], ident)
                    mm.then_inc(h1t_ps, 1)
            for part in range(2):
                a, b = PARTS[part]
                pe.wait_ge(h1_hi_done, 2 * part + 2)
                pe.wait_ge(h1_lo_done, 2 * part + 2)
                for i in range(a, b):
                    cols = slice(i * P, (i + 1) * P)
                    terms = ((h1_ahi, wr_hi, 0), (h1_alo, wr_hi, 0), (h1_ahi, wr_lo, 0),
                             (h1_bst, wr_hi, 1), (h1_bst, wr_lo, 1))
                    for k, (h, wt, r) in enumerate(terms):
                        mm = pe.matmul(bank[(6, 4)[part]][:, (i - a) * EXPERTS:(i - a + 1) * EXPERTS], h[:, cols],
                                       wt[:, r * EXPERTS:(r + 1) * EXPERTS], start=(k == 0), stop=(k == 4))
                mm.then_inc(logit_ps, 1)

            def gate_up(u):
                part, t = units[u]
                t0, n = part_range(part)
                ft = slice(t * P, (t + 1) * P)
                for which, done, used in ((0, gate_ps, gate_done), (1, up_ps, up_done)):
                    if u >= 2:
                        pe.wait_ge(used, u - 1)
                    ps = bank[2 * which + u % 2][:, 0:n]
                    terms = ((wgu_hi, 0, h1_ahi), (wgu_lo, 0, h1_ahi), (wgu_hi, 0, h1_alo),
                             (wgu_hi, 2, h1_bst), (wgu_lo, 2, h1_bst))
                    for k, (wt, r, h) in enumerate(terms):
                        mm = pe.matmul(ps, wt[:, r + which, ft], h[:, t0:t0 + n], start=(k == 0), stop=(k == 4))
                    mm.then_inc(done, 1)

            def routes(part):
                a, b = PARTS[part]
                pe.wait_ge(route_done, 3 * part + 3)
                for i in range(a, b):
                    mm = pe.transpose(bank[(7, 5)[part]][0:EXPERTS, (i - a) * P:(i - a + 1) * P],
                                      route[:, i, :], ident)
                mm.then_inc(route_ps, 1)

            def spreads(u):
                part, t = units[u]
                t0, n = part_range(part)
                if u >= 1:
                    pe.wait_ge(spread_done, u)
                pe.matmul(bank[6][:, 0:n], sel_sb[:, t * P:(t + 1) * P], route_st[:, t0:t0 + n],
                          start=True, stop=True).then_inc(spread_ps, 1)

            def down(u):
                part, t = units[u]
                a, b = PARTS[part]
                pe.wait_ge(hid_lo_done, u + 1)
                if t == 0:
                    for i in range(a, b):
                        rows = LAST if i == TILES - 1 else P
                        acc = bank[7][0:rows, i * D:(i + 1) * D] if i < 2 else \
                            bank[4 + (i - 2) // 2][0:rows, (i % 2) * D:(i % 2 + 1) * D]
                        for k, wt in enumerate((bd_hi, bd_lo)):
                            pe.matmul(acc, route_st[:, i * P:i * P + rows], wt[:],
                                      start=(k == 0 and i % 2 == 0), stop=False, skip_group_check=True)
                for i in range(a, b):
                    rows = LAST if i == TILES - 1 else P
                    acc = bank[7][0:rows, i * D:(i + 1) * D] if i < 2 else \
                        bank[4 + (i - 2) // 2][0:rows, (i % 2) * D:(i % 2 + 1) * D]
                    cols = slice((i - a) * P, (i - a) * P + rows)
                    for k, (h, wt) in enumerate(((hid_hi, wd_hi), (hid_lo, wd_hi), (hid_hi, wd_lo))):
                        mm = pe.matmul(acc, h[:, u % RING, cols], wt[:, t, :], start=False,
                                       stop=(t == FT - 1 and k == 2), skip_group_check=True)
                mm.then_inc(down_ps, 1)

            pe.wait_ge(sel_done, 1)
            for part in range(2):
                routes(part)
            pe.wait_ge(split_done, STAGES)
            for u in range(UNITS + DOWN_LAG):
                if u < UNITS:
                    if u == 0:
                        pe.wait_ge(route_lo_done, 2)
                    spreads(u)
                    gate_up(u)
                if u >= DOWN_LAG:
                    down(u - DOWN_LAG)


_OUTS = [((TOKENS, D), "float32")]


def kernel(**inputs):
    import numpy as np
    import concourse.bacc as bacc
    from concourse.bass_utils import run_bass_kernel_spmd

    x = np.asarray(inputs["x"])
    f = {k: np.asarray(v) for k, v in inputs.items()}
    side = 6
    px = 16

    patches = x.reshape(IMAGES, 3, side, px, side, px).transpose(0, 2, 4, 1, 3, 5)
    patches = patches.reshape(IMAGES, SEQ - 1, PATCH_DIM)
    patches = np.pad(patches, ((0, 0), (1, 0), (0, 0))).reshape(TOKENS, PATCH_DIM)
    x_t = patches.T.reshape(CHUNKS, P, TOKENS).transpose(1, 0, 2)
    w_emb = f["L0_tok_W_emb"].reshape(CHUNKS, P, D).transpose(1, 0, 2)

    def a_b(w):
        return np.stack([w[:P], np.concatenate([w[P:], w[P:]])], axis=1)

    def flat(w):
        return w.transpose(1, 0, 2).reshape(D, HEADS * HD)

    w_qk = np.stack([a_b(flat(f["L0_attn_Wq"])), a_b(flat(f["L0_attn_Wk"]))], axis=1)
    w_v = a_b(flat(f["L0_attn_Wv"]))
    wo = np.zeros((P, 2, D), np.float32)
    bv = np.zeros((P, 2), np.float32)
    bv_flat = f["L0_attn_bv"].reshape(-1)
    used = VH * HD
    for g in range(VG):
        r0 = VW * (g % 2)
        wo[r0:r0 + used, g // 2] = f["L0_attn_Wo"][g * used:(g + 1) * used]
        bv[r0:r0 + used, g // 2] = bv_flat[g * used:(g + 1) * used]
    wo[used, 0] = f["L0_attn_bo"]
    bv[used, 0] = 1.0

    small = np.zeros((P, SMALL), np.float32)

    def put(name, a):
        c0, c1 = COL[name]
        small[:a.shape[0], c0:c1] = a.reshape(a.shape[0], -1)

    pos = f["L0_tok_pos_embedding"][0, :SEQ].T
    for part, rows in (("a", slice(0, P)), ("b", slice(P, D))):
        put(f"pos_{part}", pos[rows])
        put(f"bemb_{part}", f["L0_tok_b_emb"][rows][:, None])
        put(f"cls_{part}", f["L0_tok_cls_token"].reshape(-1)[rows][:, None])
    for name, b in (("bq", f["L0_attn_bq"]), ("bk", f["L0_attn_bk"])):
        t = b.reshape(QG, QH * HD).T
        put(name, np.concatenate([t, t]))
    put("bv", bv)
    put("bg", f["L0_ffn_bgu"][:, :INNER].reshape(FT, P).T)
    put("bu", f["L0_ffn_bgu"][:, INNER:].reshape(FT, P).T)
    put("br", np.broadcast_to(f["L0_ffn_br"], (P, EXPERTS)))
    wr = a_b(f["L0_ffn_Wr"])
    put("wr_a", wr[:, 0])
    put("wr_b", wr[:, 1])
    rows = np.arange(P)
    put("head_mask", (rows[:, None] % DB // HD == np.arange(QH)).astype(np.float32))
    keys = np.arange(KEYS)
    put("value_mask", (keys[:, None] // SEQ == np.arange(VH * HD) // HD).astype(np.float32))
    queries = np.arange(PAIR_TOKENS) % SEQ
    put("causal", np.where(np.arange(SEQ) > queries[:, None], MASKED, 0.0).astype(np.float32))
    put("ident", np.eye(P, dtype=np.float32))
    bd = np.zeros((40, D), np.float32)
    bd[0:EXPERTS] = f["L0_ffn_bd"]
    bd[32:40] = f["L0_ffn_bd"]
    put("bd", bd)

    owner = np.arange(EXPERTS * INNER) // INNER
    sel = np.zeros((40, FT * P), np.float32)
    sel[owner, np.arange(FT * P)] = 1.0
    sel[32 + owner, np.arange(FT * P)] = 1.0

    wgu = f["L0_ffn_Wgu"].transpose(1, 0, 2)
    g_ab = a_b(wgu[:, :, :INNER].reshape(D, FT * P))
    u_ab = a_b(wgu[:, :, INNER:].reshape(D, FT * P))
    w_gu = np.stack([g_ab[:, 0], u_ab[:, 0], g_ab[:, 1], u_ab[:, 1]], axis=1)
    w_d = f["L0_ffn_Wd"].reshape(FT, P, D).transpose(1, 0, 2).reshape(P, FT * D)

    nc = bacc.Bacc("TRN2", target_bir_lowering=False, num_devices=1)
    arrays, args = {}, []
    for name, a in (("x_t", x_t), ("w_emb", w_emb), ("small", small), ("w_qk", w_qk), ("w_v", w_v),
                    ("w_o", wo), ("sel", sel), ("w_gu", w_gu), ("w_d", w_d)):
        arrays[name] = np.ascontiguousarray(a)
        args.append(nc.dram_tensor(name, a.shape, mybir.dt.from_np(a.dtype), kind="ExternalInput").ap())
    args.append(nc.dram_tensor("out_0", (TOKENS, D), F32, kind="ExternalOutput").ap())
    build_program(nc, *args)
    r = run_bass_kernel_spmd(nc, [arrays], core_ids=[0])
    return r.results[0]["out_0"].reshape(IMAGES, SEQ, D)
```

```python
from contextlib import ExitStack

import concourse.bass as bass
from concourse import mybir

F32 = mybir.dt.float32
F32R = mybir.dt.float32r
BF16 = mybir.dt.bfloat16
U32 = mybir.dt.uint32
ALU = mybir.AluOpType
ACT = mybir.ActivationFunctionType
AX_X = mybir.AxisListType.X

P = 128
IMAGES, SEQ, D = 16, 37, 192
TOKENS = IMAGES * SEQ
HALF = TOKENS // 2
DB = D - P
PATCH_DIM = 768
CHUNKS = PATCH_DIM // P
HEADS, HD = 12, 16
PAIRS, MEMBERS = IMAGES // 2, 2
QG = 3
QH = HEADS // QG
VG = 4
VH = HEADS // VG
VW = 64
PAIR_TOKENS = MEMBERS * SEQ
SCORES = HEADS * SEQ
KEYS = VH * SEQ
EXPERTS, INNER = 8, 192
FT = EXPERTS * INNER // P
TILES = 5
PADDED = TILES * P
LAST = TOKENS - (TILES - 1) * P
PARTS = [(0, 2), (2, 5)]
X_RING = 4
LOTS = 6
TL = FT // LOTS
LOT_GU = TL * P
LOT = 4 * LOT_GU + TL * D
PIECES = 2 * LOTS
PIECE = LOT // 2
ATT_SCALE = 0.25
ALPHA, LIMIT, EPS = 1.702, 7.0, 1e-5
MASKED = -1e37

_COLS = [("pos_a", SEQ), ("pos_b", SEQ), ("bemb_a", 1), ("bemb_b", 1), ("cls_a", 1), ("cls_b", 1),
         ("bq", QG), ("bk", QG), ("bv", 2), ("bg", FT), ("bu", FT), ("br", EXPERTS),
         ("wr_a", EXPERTS), ("wr_b", EXPERTS), ("head_mask", QH), ("value_mask", VH * HD),
         ("causal", SEQ), ("ident", P), ("bd", D)]
COL = {}
_at = 0
for _name, _n in _COLS:
    COL[_name] = (_at, _at + _n)
    _at += _n
SMALL = _at


def part_range(part):
    a, b = PARTS[part]
    return a * P, min(b * P, TOKENS) - a * P


def build_program(nc, x_t, w_emb, small, w_qk, w_v, w_o, sel, w_experts, out):
    with ExitStack() as ctx:
        def sb(stack, name, shape, dt=F32):
            return stack.enter_context(nc.sbuf_tensor(name, shape, dt))

        def sem(name):
            return ctx.enter_context(nc.semaphore(name))

        sm = sb(ctx, "sm", [P, SMALL])
        ident_bf = sb(ctx, "ident_bf", [P, P], BF16)
        causal_bf = sb(ctx, "causal_bf", [P, SEQ], BF16)
        bu1 = sb(ctx, "bu1", [P, FT])
        eps = sb(ctx, "eps", [P, 1])
        expert_ids = sb(ctx, "expert_ids", [P, EXPERTS])
        wr_hi = sb(ctx, "wr_hi", [P, 2 * EXPERTS], F32R)
        wr_lo = sb(ctx, "wr_lo", [P, 2 * EXPERTS], F32R)
        bd_hi = sb(ctx, "bd_hi", [40, D], F32R)
        bd_lo = sb(ctx, "bd_lo", [40, D], F32R)
        res_a = sb(ctx, "res_a", [P, PADDED])
        res_b = sb(ctx, "res_b", [DB, PADDED])
        wo_sb = sb(ctx, "wo_sb", [P, 2, D])
        h1 = sb(ctx, "h1", [P, TILES, D])
        h1_ahi = sb(ctx, "h1_ahi", [P, PADDED], F32R)
        h1_alo = sb(ctx, "h1_alo", [P, PADDED], F32R)
        h1_bst = sb(ctx, "h1_bst", [P, PADDED], F32R)
        stats = sb(ctx, "stats", [P, TILES, 6])
        mv = sb(ctx, "mv", [P, TILES, 2])
        std = sb(ctx, "std", [P, TILES])
        rstd = sb(ctx, "rstd", [P, TILES])
        logits = sb(ctx, "logits", [P, TILES, EXPERTS])
        top = sb(ctx, "top", [P, TILES, EXPERTS])
        top_id = sb(ctx, "top_id", [P, TILES, EXPERTS], U32)
        top_idf = sb(ctx, "top_idf", [P, TILES, 2])
        gap = sb(ctx, "gap", [P, TILES])
        share = sb(ctx, "share", [P, 2, TILES])
        pick = sb(ctx, "pick", [P, 2, TILES, EXPERTS])
        route = sb(ctx, "route", [P, TILES, EXPERTS])
        route_st = sb(ctx, "route_st", [40, PADDED], F32R)
        sel_sb = sb(ctx, "sel_sb", [40, FT * P], F32R)
        warm = sb(ctx, "warm", [P, 1])
        stage = sb(ctx, "stage", [P, 2, LOT])

        with ExitStack() as early:
            x_hi = sb(early, "x_hi", [P, X_RING, TOKENS], F32R)
            x_lo = sb(early, "x_lo", [P, X_RING, TOKENS], F32R)
            x_raw = sb(early, "x_raw", [P, CHUNKS, TOKENS])
            we_raw = sb(early, "we_raw", [P, CHUNKS, D])
            we_hi = sb(early, "we_hi", [P, CHUNKS, D], F32R)
            we_lo = sb(early, "we_lo", [P, CHUNKS, D], F32R)
            sel_raw = sb(early, "sel_raw", [40, FT * P])
            wqk_raw = sb(early, "wqk_raw", [P, 2, 2, D])
            wv_raw = sb(early, "wv_raw", [P, 2, D])
        experts_hi = sb(ctx, "experts_hi", [P, LOTS, LOT], F32R)
        experts_lo = sb(ctx, "experts_lo", [P, LOTS, LOT], F32R)
        ctx_t = sb(ctx, "ctx_t", [P, 2, PADDED])

        with ExitStack() as att:
            keys = sb(att, "keys", [P, QG, PAIRS, QH, SEQ])
            values = sb(att, "values", [KEYS, MEMBERS, PAIRS, VG, VW])
            h_ahi = sb(att, "h_ahi", [P, TOKENS], F32R)
            h_alo = sb(att, "h_alo", [P, TOKENS], F32R)
            h_bst = sb(att, "h_bst", [P, TOKENS], F32R)
            all_keys = sb(att, "all_keys", [P, 2, PAIRS, SEQ])
            queries = sb(att, "queries", [P, QG, PAIRS, PAIR_TOKENS])
            rep = [sb(att, f"rep_{n}", [P, IMAGES, VH, SEQ], F32R) for n in ("ahi", "alo", "bst")]
            wv_hi = sb(att, "wv_hi", [P, 2, D], F32R)
            wv_lo = sb(att, "wv_lo", [P, 2, D], F32R)
            with ExitStack() as proj:
                wqk_hi = sb(proj, "wqk_hi", [P, 2, 2, QG, 3 * DB], F32R)
                wqk_lo = sb(proj, "wqk_lo", [P, 2, 2, QG, 3 * DB], F32R)
            shifted = sb(att, "shifted", [PAIR_TOKENS, 2, SCORES])
            expd = sb(att, "expd", [PAIR_TOKENS, 2, SCORES])
            probs = sb(att, "probs", [PAIR_TOKENS, 2, SCORES])
            probs_t = sb(att, "probs_t", [KEYS, 2, VG, PAIR_TOKENS])
            top_score = sb(att, "top_score", [PAIR_TOKENS, 2, HEADS])
            prob_sum = sb(att, "prob_sum", [PAIR_TOKENS, 2, HEADS])
            prob_inv = sb(att, "prob_inv", [PAIR_TOKENS, 2, HEADS])
        NMAX = part_range(1)[1]
        RING = 6
        gate = sb(ctx, "gate", [P, RING, NMAX])
        up = sb(ctx, "up", [P, RING, NMAX])
        sig = sb(ctx, "sig", [P, RING, NMAX])
        spread = sb(ctx, "spread", [P, RING, NMAX])
        sig_w = sb(ctx, "sig_w", [P, RING, NMAX])
        glu = sb(ctx, "glu", [P, RING, NMAX])
        hid = sb(ctx, "hid", [P, RING, NMAX])
        hid_hi = sb(ctx, "hid_hi", [P, RING, NMAX], F32R)
        hid_lo = sb(ctx, "hid_lo", [P, RING, NMAX], F32R)
        y2 = sb(ctx, "y2", [P, TILES, D])
        result = sb(ctx, "result", [P, TILES, D])

        bank = [ctx.enter_context(nc.psum_tensor(f"bank{i}", [P, 512], F32)) for i in range(8)]

        x_in = [sem(f"x_in{c}") for c in range(CHUNKS)]
        we_first_in, we_in, small_in, wqk_in, wv_in, wo_in, sel_in = (
            sem(n) for n in ("we_first_in", "we_in", "small_in", "wqk_in", "wv_in", "wo_in", "sel_in"))
        stage_in = [sem(f"stage_in{i}") for i in range(LOTS)]
        out_done = [sem(f"out_done{i}") for i in range(TILES)]
        warm_done = sem("warm_done")
        pool_zero = sem("pool_zero")
        prep_done = sem("prep_done")
        x_hi_done, x_lo_done = sem("x_hi_done"), sem("x_lo_done")
        we_hi_done, we_lo_done = sem("we_hi_done"), sem("we_lo_done")
        emb_chunk, emb_done = sem("emb_chunk"), sem("emb_done")
        res_done, h_hi_done, h_lo_done = sem("res_done"), sem("h_hi_done"), sem("h_lo_done")
        wqk_hi_done, wqk_lo_done = sem("wqk_hi_done"), sem("wqk_lo_done")
        qk_ps, q_done, k_done, all_keys_done = (sem(n) for n in ("qk_ps", "q_done", "k_done", "all_keys_done"))
        rep_done, v_ps, v_done = sem("rep_done"), sem("v_ps"), sem("v_done")
        scores_ps, top_done, shift_done, exp_done = (
            sem(n) for n in ("scores_ps", "top_done", "shift_done", "exp_done"))
        sum_done, inv_done, probs_done = sem("sum_done"), sem("inv_done"), sem("probs_done")
        probs_ps, probs_t_done, ctx_ps, ctx_done = (
            sem(n) for n in ("probs_ps", "probs_t_done", "ctx_ps", "ctx_done"))
        y_ps, stats_done, mv_done, std_done, rstd_done, h1_done = (
            sem(n) for n in ("y_ps", "stats_done", "mv_done", "std_done", "rstd_done", "h1_done"))
        h1t_ps, h1_hi_done, h1_lo_done = sem("h1t_ps"), sem("h1_hi_done"), sem("h1_lo_done")
        logit_ps, router, share_done, route_done = (
            sem(n) for n in ("logit_ps", "router", "share_done", "route_done"))
        route_ps, route_hi_done, route_lo_done = (
            sem(n) for n in ("route_ps", "route_hi_done", "route_lo_done"))
        split_hi, split_done = sem("split_hi"), sem("split_done")
        wv_hi_done, wv_lo_done, sel_done = sem("wv_hi_done"), sem("wv_lo_done"), sem("sel_done")
        spread_ps, gate_ps, up_ps = sem("spread_ps"), sem("gate_ps"), sem("up_ps")
        spread_done, gate_done, up_done, sig_done = (
            sem(n) for n in ("spread_done", "gate_done", "up_done", "sig_done"))
        sigw_done, glu_done, hid_done = sem("sigw_done"), sem("glu_done"), sem("hid_done")
        hid_hi_done, hid_lo_done, down_ps = sem("hid_hi_done"), sem("hid_lo_done"), sem("down_ps")
        y2_done, stats2_done, mv2_done, std2_done, rstd2_done, result_done = (
            sem(n) for n in ("y2_done", "stats2_done", "mv2_done", "std2_done", "rstd2_done", "result_done"))

        def col(name, rows=P):
            a, b = COL[name]
            return sm[0:rows, a:b]

        units = [(part, t) for part in range(2) for t in range(FT)]
        UNITS = len(units)
        SPREAD_LAG, HIDDEN_LAG, LO_LAG, DOWN_LAG = 2, 3, 4, 5

        def tiles_down(u):
            return sum(PARTS[part][1] - PARTS[part][0] for part, _ in units[:u + 1])

        def acc(i):
            rows = LAST if i == TILES - 1 else P
            b, j = (7, i) if i < 2 else (4 + (i - 2) // 2, i % 2)
            return bank[b][0:rows, j * D:(j + 1) * D]

        def expert_weights(t, half):
            at = (t % TL) * P
            return [slice((2 * r + half) * LOT_GU + at, (2 * r + half) * LOT_GU + at + P) for r in range(2)]

        def down_weights(t):
            at = 4 * LOT_GU + (t % TL) * D
            return slice(at, at + D)

        Y_BANK = (6, 4, 7, 5, 4)
        H1T_BANK = ((0, 2), (5, 4))
        ROUTER_BANK = (7, 5)

        PREP = 21

        def slots(t, half):
            return t.rearrange("d (m p k) -> d p m k", m=MEMBERS, p=PAIRS)[:, 4 * half:4 * half + 4]

        def qk_bank(g, w):
            return bank[(4 + 2 * g + w) % 8][:, 0:HALF].rearrange("d (p k) -> d p k", p=PAIRS)

        def by_pair(t):
            return t.rearrange("d (p m k) -> d p m k", p=PAIRS // 2, m=MEMBERS)

        block = ctx.enter_context(nc.Block())

        @block.sync
        def _(sp):
            sp.dma_start(we_raw[:, 0, :], w_emb[:, 0, :]).then_inc(we_first_in, 16)
            for c in range(CHUNKS):
                sp.dma_start(x_raw[:, c, :], x_t[:, c, :]).then_inc(x_in[c], 16)
                if c == 0:
                    sp.dma_start(we_raw[:, 1:, :], w_emb[:, 1:, :]).then_inc(we_in, 16)
                if c == 2:
                    sp.dma_start(sm[:], small).then_inc(small_in, 16)
                if c == 4:
                    sp.dma_start(wqk_raw[:], w_qk).then_inc(wqk_in, 16)
            sp.dma_start(wv_raw[:], w_v).then_inc(wv_in, 16)
            sp.dma_start(sel_raw[:], sel).then_inc(sel_in, 16)
            for i in range(LOTS):
                if i >= 2:
                    sp.wait_ge(split_done, 2 * (i - 1))
                sp.dma_start(stage[:, i % 2, :], w_experts[:, i, :]).then_inc(stage_in[i], 16)
                if i == 1:
                    sp.dma_start(wo_sb[:], w_o).then_inc(wo_in, 16)
            for i in range(TILES):
                rows = LAST if i == TILES - 1 else P
                sp.wait_ge(result_done, i + 1)
                sp.dma_start(out[i * P:i * P + rows, :], result[0:rows, i, :]).then_inc(out_done[i], 16)
            for i in range(TILES):
                sp.wait_ge(out_done[i], 16)

        @block.gpsimd
        def _(pool):
            pool.memset(wqk_hi[:].bitcast(F32), 0.0).then_inc(pool_zero, 1)
            for c in range(CHUNKS):
                pool.wait_ge(we_first_in if c == 0 else we_in, 16)
                pool.tensor_scalar(we_hi[:, c, :], we_raw[:, c, :], 1.0, 1.0, ALU.mult, ALU.mult)\
                    .then_inc(we_hi_done, 1)
                pool.wait_ge(we_hi_done, c + 1)
                pool.tensor_tensor(we_lo[:, c, :], we_raw[:, c, :], we_hi[:, c, :].bitcast(F32),
                                   ALU.subtract).then_inc(we_lo_done, 1)
            pool.memset(wqk_lo[:].bitcast(F32), 0.0).then_inc(pool_zero, 1)
            pool.wait_ge(wqk_in, 16)
            pool.wait_ge(pool_zero, 2)
            for w in range(2):
                for r in range(2):
                    dst = wqk_hi[:, w, r, :, DB:2 * DB]
                    src = wqk_raw[:, w, r, :].rearrange("p (g c) -> p g c", g=QG)
                    pool.tensor_scalar(dst, src, 1.0, 1.0, ALU.mult, ALU.mult).then_inc(wqk_hi_done, 1)
                    pool.wait_ge(wqk_hi_done, 2 * w + r + 1)
                    pool.tensor_tensor(wqk_lo[:, w, r, :, DB:2 * DB], src, dst.bitcast(F32),
                                       ALU.subtract).then_inc(wqk_lo_done, 1)
            pool.memset(queries[:], 0.0).then_inc(pool_zero, 1)
            srcs = (h_ahi, h_alo, h_bst)
            for i, (dst, src) in enumerate(zip(rep, srcs)):
                if i == 0:
                    pool.wait_ge(h_hi_done, 4)
                    pool.wait_ge(h_lo_done, 4)
                view = src[:].bitcast(F32).rearrange("d (s k) -> d s k", s=IMAGES)
                pool.tensor_scalar(dst[:], view.unsqueeze(2).broadcast_to([P, IMAGES, VH, SEQ]), 1.0, 1.0,
                                   ALU.mult, ALU.mult).then_inc(rep_done, 1)
            pool.memset(values[:, :, :, :, VH * HD:VW], 0.0).then_inc(pool_zero, 1)
            pool.memset(ctx_t[:, :, TOKENS:PADDED], 0.0).then_inc(pool_zero, 1)

            def split_lo(k):
                lot, cols = k // 2, slice(k % 2 * PIECE, (k % 2 + 1) * PIECE)
                pool.wait_ge(split_hi, k + 1)
                pool.tensor_tensor(experts_lo[:, lot, cols], stage[:, lot % 2, cols],
                                   experts_hi[:, lot, cols].bitcast(F32), ALU.subtract).then_inc(split_done, 1)

            split_lo(0)
            split_lo(1)
            for p in range(PAIRS):
                pool.wait_ge(exp_done, p + 1)
                pool.wait_ge(inv_done, p + 1)
                if p >= 2:
                    pool.wait_ge(probs_ps, p - 1)
                pool.tensor_tensor(
                    probs[:, p % 2, :].rearrange("q (h k) -> q h k", h=HEADS),
                    expd[:, p % 2, :].rearrange("q (h k) -> q h k", h=HEADS),
                    prob_inv[:, p % 2, :].unsqueeze(2).broadcast_to([PAIR_TOKENS, HEADS, SEQ]),
                    ALU.mult).then_inc(probs_done, 1)
                split_lo(p + 2)
            split_lo(PIECES - 2)
            split_lo(PIECES - 1)
            for u, (part, t) in enumerate(units):
                n = part_range(part)[1]
                r = u % RING
                pool.wait_ge(sig_done, u + 1)
                pool.wait_ge(spread_done, u + 1)
                pool.tensor_tensor(sig_w[:, r, 0:n], sig[:, r, 0:n], spread[:, r, 0:n], ALU.mult)\
                    .then_inc(sigw_done, 1)
                pool.wait_ge(sigw_done, u + 1)
                if u >= RING:
                    pool.wait_ge(hid_done, u - RING + 1)
                pool.tensor_tensor(glu[:, r, 0:n], sig_w[:, r, 0:n], gate[:, r, 0:n], ALU.mult)\
                    .then_inc(glu_done, 1)

        @block.scalar
        def _(act):
            def deviations(*tiles):
                for i in tiles:
                    act.wait_ge(mv_done, i + 1)
                    act.activation(std[:, i:i + 1], mv[:, i, 1:2], ACT.Sqrt, bias=eps[:]).then_inc(std_done, 1)

            def h1_rounded(part):
                c0 = PARTS[part][0] * P
                n = (PARTS[part][1] - PARTS[part][0]) * P
                bank_a, bank_b = H1T_BANK[part]
                act.wait_ge(h1t_ps, 2 * part + 1)
                act.activation(h1_ahi[:, c0:c0 + n], bank[bank_a][:, 0:n], ACT.Copy).then_inc(h1_hi_done, 1)
                act.wait_ge(h1t_ps, 2 * part + 2)
                act.activation(h1_bst[0:DB, c0:c0 + n], bank[bank_b][0:DB, 0:n], ACT.Copy)\
                    .then_inc(h1_hi_done, 1)

            def shares(part):
                a, b = PARTS[part]
                act.wait_ge(router, 5 * part + 4)
                for k, sign in ((0, 1.0), (1, -1.0)):
                    act.activation(share[:, k, a:b], gap[:, a:b], ACT.Sigmoid, scale=sign).then_inc(share_done, 1)

            def route_rounded(part):
                a, b = PARTS[part]
                act.wait_ge(route_ps, part + 1)
                act.activation(route_st[0:EXPERTS, a * P:b * P],
                               bank[ROUTER_BANK[part]][0:EXPERTS, 0:(b - a) * P],
                               ACT.Copy).then_inc(route_hi_done, 1)

            act.wait_ge(prep_done, 1)
            act.activation(warm[:], eps[:], ACT.Exp).then_inc(warm_done, 1)
            for c in range(CHUNKS):
                act.wait_ge(x_in[c], 16)
                if c >= X_RING:
                    act.wait_ge(emb_chunk, c - X_RING + 1)
                act.activation(x_hi[:, c % X_RING, :], x_raw[:, c, :], ACT.Copy).then_inc(x_hi_done, 1)
            act.wait_ge(wv_in, 16)
            act.activation(wv_hi[:], wv_raw[:], ACT.Copy).then_inc(wv_hi_done, 1)
            for half in range(2):
                cols = slice(half * HALF, (half + 1) * HALF)
                act.wait_ge(res_done, 2 * half + 1)
                act.activation(slots(h_ahi[:], half), by_pair(res_a[:, cols]), ACT.Copy).then_inc(h_hi_done, 1)
                act.wait_ge(res_done, 2 * half + 2)
                act.activation(slots(h_bst[0:DB, :], half), by_pair(res_b[:, cols]), ACT.Copy)\
                    .then_inc(h_hi_done, 1)
            act.wait_ge(pool_zero, 3)
            for g in range(QG):
                act.wait_ge(qk_ps, 2 * g + 1)
                src = qk_bank(g, 0)
                for m in range(MEMBERS):
                    rows = slice(m * DB, (m + 1) * DB)
                    act.activation(queries[rows, g, :, m * SEQ:(m + 1) * SEQ], src[rows], ACT.Identity,
                                   bias=sm[rows, COL["bq"][0] + g:COL["bq"][0] + g + 1]).then_inc(q_done, 1)
                act.wait_ge(qk_ps, 2 * g + 2)
                if g >= 2:
                    act.wait_ge(k_done, QH * (g - 1))
                act.activation(all_keys[:, g % 2], qk_bank(g, 1), ACT.Identity,
                               bias=sm[:, COL["bk"][0] + g:COL["bk"][0] + g + 1]).then_inc(all_keys_done, 1)
            act.wait_ge(sel_in, 16)
            act.activation(sel_sb[:], sel_raw[:], ACT.Copy).then_inc(sel_done, 1)

            def split_hi_piece(k):
                lot, cols = k // 2, slice(k % 2 * PIECE, (k % 2 + 1) * PIECE)
                act.wait_ge(stage_in[lot], 16)
                act.activation(experts_hi[:, lot, cols], stage[:, lot % 2, cols], ACT.Copy).then_inc(split_hi, 1)

            act.wait_ge(emb_done, 4)
            act.wait_ge(wqk_lo_done, 4)
            act.wait_ge(wv_lo_done, 1)
            act.wait_ge(sel_done, 1)
            split_hi_piece(0)
            split_hi_piece(1)
            for p in range(PAIRS + 3):
                if p < PAIRS:
                    act.wait_ge(shift_done, p + 1)
                    if p >= 2:
                        act.wait_ge(probs_done, p - 1)
                    act.activation(expd[:, p % 2, :], shifted[:, p % 2, :], ACT.Exp, scale=ATT_SCALE)\
                        .then_inc(exp_done, 1)
                if p + 2 < PIECES:
                    split_hi_piece(p + 2)
                if 2 <= p < PAIRS + 2:
                    q = p - 2
                    act.wait_ge(probs_ps, q + 1)
                    if q >= 2:
                        act.wait_ge(ctx_ps, q - 1)
                    act.activation(probs_t[:, q % 2].rearrange("k g q -> k (g q)"),
                                   bank[q % 2][0:KEYS, 0:VG * PAIR_TOKENS], ACT.Copy)\
                        .then_inc(probs_t_done, 1)
                if p >= 3:
                    q = p - 3
                    act.wait_ge(ctx_ps, q + 1)
                    for c in range(2):
                        act.activation(ctx_t[:, c, q * PAIR_TOKENS:(q + 1) * PAIR_TOKENS],
                                       bank[2 + q % 2][:, c * PAIR_TOKENS:(c + 1) * PAIR_TOKENS], ACT.Identity,
                                       bias=sm[:, COL["bv"][0] + c:COL["bv"][0] + c + 1]).then_inc(ctx_done, 1)
                if p == PAIRS + 1:
                    deviations(0, 1)
            deviations(2, 3)
            h1_rounded(0)
            deviations(4)

            def hidden_hi(u):
                n = part_range(units[u][0])[1]
                r = u % RING
                act.wait_ge(hid_done, u + 1)
                if u >= RING:
                    act.wait_ge(down_ps, tiles_down(u - RING))
                act.activation(hid_hi[:, r, 0:n], hid[:, r, 0:n], ACT.Copy).then_inc(hid_hi_done, 1)

            for u in range(UNITS + HIDDEN_LAG):
                if u < UNITS:
                    part, t = units[u]
                    n = part_range(part)[1]
                    r = u % RING
                    act.wait_ge(gate_done, u + 1)
                    if u >= RING:
                        act.wait_ge(sigw_done, u - RING + 1)
                    act.activation(sig[:, r, 0:n], gate[:, r, 0:n], ACT.Sigmoid, scale=ALPHA)\
                        .then_inc(sig_done, 1)
                if u == 0:
                    shares(0)
                if u == 1:
                    h1_rounded(1)
                    route_rounded(0)
                if u == 2:
                    shares(1)
                if u == 3:
                    route_rounded(1)
                if SPREAD_LAG <= u < UNITS + SPREAD_LAG:
                    v = u - SPREAD_LAG
                    n = part_range(units[v][0])[1]
                    r = v % RING
                    act.wait_ge(spread_ps, v + 1)
                    if v >= RING:
                        act.wait_ge(sigw_done, v - RING + 1)
                    act.activation(spread[:, r, 0:n], bank[6][:, 0:n], ACT.Copy).then_inc(spread_done, 1)
                if u == UNITS + 1:
                    act.wait_ge(mv2_done, 2)
                    act.activation(std[:, 0:2], mv[:, 0:2, 1], ACT.Sqrt, bias=eps[:]).then_inc(std2_done, 1)
                if u >= HIDDEN_LAG:
                    hidden_hi(u - HIDDEN_LAG)
            act.wait_ge(mv2_done, TILES)
            act.activation(std[:, 2:TILES], mv[:, 2:TILES, 1], ACT.Sqrt, bias=eps[:]).then_inc(std2_done, 1)

        @block.vector
        def _(dve):
            dve.memset(eps[:], EPS).then_inc(prep_done, 1)
            dve.memset(route_st[:].bitcast(F32), 0.0).then_inc(prep_done, 1)
            dve.memset(res_a[:, TOKENS:PADDED], 0.0).then_inc(prep_done, 1)
            dve.memset(res_b[:, TOKENS:PADDED], 0.0).then_inc(prep_done, 1)
            for e in range(EXPERTS):
                dve.memset(expert_ids[:, e:e + 1], float(e)).then_inc(prep_done, 1)
            def small_operands():
                dve.wait_ge(small_in, 16)
                for part, rows in (("a", P), ("b", DB)):
                    pos, bias, cls = (col(f"{n}_{part}", rows) for n in ("pos", "bemb", "cls"))
                    dve.tensor_scalar(pos[:, 1:SEQ], pos[:, 1:SEQ], bias, None, ALU.add).then_inc(prep_done, 1)
                    dve.tensor_scalar(pos[:, 0:1], pos[:, 0:1], cls, None, ALU.add).then_inc(prep_done, 1)
                dve.tensor_copy(ident_bf[:], col("ident")).then_inc(prep_done, 1)
                dve.tensor_copy(causal_bf[:], col("causal")).then_inc(prep_done, 1)
                dve.tensor_scalar(bu1[:], col("bu"), 1.0, None, ALU.add).then_inc(prep_done, 1)
                wr = sm[:, COL["wr_a"][0]:COL["wr_b"][1]]
                dve.tensor_copy(wr_hi[:], wr).then_inc(prep_done, 1)
                dve.tensor_copy(bd_hi[:], col("bd", 40)).then_inc(prep_done, 1)
                dve.wait_ge(prep_done, PREP)
                dve.tensor_tensor(wr_lo[:], wr, wr_hi[:].bitcast(F32), ALU.subtract).then_inc(prep_done, 1)
                dve.tensor_tensor(bd_lo[:], col("bd", 40), bd_hi[:].bitcast(F32), ALU.subtract)\
                    .then_inc(prep_done, 1)

            for c in range(CHUNKS):
                dve.wait_ge(x_hi_done, c + 1)
                if c >= X_RING:
                    dve.wait_ge(emb_chunk, c - X_RING + 1)
                dve.tensor_tensor(x_lo[:, c % X_RING, :], x_raw[:, c, :], x_hi[:, c % X_RING, :].bitcast(F32),
                                  ALU.subtract).then_inc(x_lo_done, 1)
                if c == 2:
                    small_operands()
            dve.wait_ge(wv_hi_done, 1)
            dve.tensor_tensor(wv_lo[:], wv_raw[:], wv_hi[:].bitcast(F32), ALU.subtract)\
                .then_inc(wv_lo_done, 1)
            for half in range(2):
                cols = slice(half * HALF, (half + 1) * HALF)
                for r, (res, rows, part) in enumerate(((res_a, P, "a"), (res_b, DB, "b"))):
                    dve.wait_ge(emb_done, 2 * half + r + 1)
                    dve.tensor_tensor(
                        res[:, cols].rearrange("d (b k) -> d b k", k=SEQ),
                        bank[2 * r + half][0:rows, 0:HALF].rearrange("d (b k) -> d b k", k=SEQ),
                        col(f"pos_{part}", rows).unsqueeze(1).broadcast_to([rows, IMAGES // 2, SEQ]),
                        ALU.add).then_inc(res_done, 1)
            for half in range(2):
                cols = slice(half * HALF, (half + 1) * HALF)
                dve.wait_ge(res_done, 2 * half + 2)
                dve.wait_ge(h_hi_done, 2 * half + 1)
                dve.tensor_tensor(slots(h_alo[:], half), by_pair(res_a[:, cols]),
                                  slots(h_ahi[:].bitcast(F32), half), ALU.subtract).then_inc(h_lo_done, 1)
                dve.wait_ge(h_hi_done, 2 * half + 2)
                dve.tensor_tensor(slots(h_bst[DB:P, :], half), by_pair(res_b[:, cols]),
                                  slots(h_bst[0:DB, :].bitcast(F32), half), ALU.subtract)\
                    .then_inc(h_lo_done, 1)
            for g in range(QG):
                dve.wait_ge(all_keys_done, g + 1)
                for h in range(QH):
                    keep = sm[:, COL["head_mask"][0] + h:COL["head_mask"][0] + h + 1]
                    dve.tensor_scalar(keys[:, g, :, h, :], all_keys[:, g % 2], keep, None, ALU.mult)\
                        .then_inc(k_done, 1)

            def value_rows(p):
                dve.wait_ge(v_ps, p + 1)
                if p == 0:
                    dve.wait_ge(pool_zero, 4)
                src = bank[4 + p % 2][0:KEYS, 0:MEMBERS * D].rearrange("k (s c) -> k s c", c=VH * HD)
                keep = col("value_mask", KEYS).unsqueeze(1).broadcast_to([KEYS, MEMBERS * VG, VH * HD])
                dst = values[:, :, p, :, 0:VH * HD]
                dve.tensor_tensor(dst, src.rearrange("k (m g) c -> k m g c", m=MEMBERS),
                                  keep.rearrange("k (m g) c -> k m g c", m=MEMBERS), ALU.mult)\
                    .then_inc(v_done, 1)

            def by_head(t):
                return t.rearrange("q (h k) -> q h k", h=HEADS)

            def pair_step(p):
                if p < PAIRS:
                    src = by_head(bank[6 + p % 2][0:PAIR_TOKENS, 0:SCORES])
                    dve.wait_ge(scores_ps, p + 1)
                    dve.tensor_reduce(top_score[:, p % 2, :], src, AX_X, ALU.max).then_inc(top_done, 1)
                if p >= 1:
                    q = p - 1
                    dve.wait_ge(exp_done, q + 1)
                    dve.tensor_reduce(prob_sum[:, q % 2, :], by_head(expd[:, q % 2, :]), AX_X, ALU.add)\
                        .then_inc(sum_done, 1)
                if p < PAIRS:
                    dve.wait_ge(top_done, p + 1)
                    if p >= 2:
                        dve.wait_ge(exp_done, p - 1)
                    dve.tensor_tensor(by_head(shifted[:, p % 2, :]), src,
                                      top_score[:, p % 2, :].unsqueeze(2).broadcast_to([PAIR_TOKENS, HEADS, SEQ]),
                                      ALU.subtract).then_inc(shift_done, 1)
                if p >= 1:
                    dve.wait_ge(sum_done, q + 1)
                    if q >= 2:
                        dve.wait_ge(probs_done, q - 1)
                    dve.reciprocal(prob_inv[:, q % 2, :], prob_sum[:, q % 2, :]).then_inc(inv_done, 1)

            for p in range(PAIRS + 1):
                pair_step(p)
                if p >= 1:
                    value_rows(p - 1)

            def norm_stats(i):
                dve.wait_ge(y_ps, i + 1)
                dve.bn_stats(stats[:, i, :], bank[Y_BANK[i]][:, 0:D]).then_inc(stats_done, 1)
                dve.wait_ge(stats_done, i + 1)
                dve.bn_aggr(mv[:, i, :], stats[:, i, :]).then_inc(mv_done, 1)

            def norm_apply(i):
                dve.wait_ge(std_done, i + 1)
                dve.reciprocal(rstd[:, i:i + 1], std[:, i:i + 1]).then_inc(rstd_done, 1)
                dve.wait_ge(rstd_done, i + 1)
                dve.wait_ge(mv_done, i + 1)
                dve.tensor_scalar(h1[:, i, :], bank[Y_BANK[i]][:, 0:D], mv[:, i, 0:1], rstd[:, i:i + 1],
                                  ALU.subtract, ALU.mult).then_inc(h1_done, 1)

            def h1_rests(part):
                c0 = PARTS[part][0] * P
                n = (PARTS[part][1] - PARTS[part][0]) * P
                bank_a, bank_b = H1T_BANK[part]
                dve.wait_ge(h1_hi_done, 2 * part + 1)
                dve.tensor_tensor(h1_alo[:, c0:c0 + n], bank[bank_a][:, 0:n],
                                  h1_ahi[:, c0:c0 + n].bitcast(F32), ALU.subtract).then_inc(h1_lo_done, 1)
                dve.wait_ge(h1_hi_done, 2 * part + 2)
                dve.tensor_tensor(h1_bst[DB:P, c0:c0 + n], bank[bank_b][0:DB, 0:n],
                                  h1_bst[0:DB, c0:c0 + n].bitcast(F32), ALU.subtract).then_inc(h1_lo_done, 1)

            norm_stats(0)
            norm_stats(1)
            norm_apply(0)
            norm_stats(2)
            norm_apply(1)
            norm_stats(3)
            norm_apply(2)
            norm_apply(3)
            h1_rests(0)
            norm_stats(4)
            norm_apply(4)

            def choose(part):
                a, b = PARTS[part]
                n = b - a
                r0 = 5 * part
                dve.wait_ge(logit_ps, part + 1)
                dve.tensor_tensor(logits[:, a:b, :],
                                  bank[ROUTER_BANK[part]][:, 0:n * EXPERTS].rearrange("t (i e) -> t i e", e=EXPERTS),
                                  col("br").unsqueeze(1).broadcast_to([P, n, EXPERTS]), ALU.add)\
                    .then_inc(router, 1)
                dve.wait_ge(router, r0 + 1)
                for i in range(a, b):
                    ins = dve.max(top[:, i, :], logits[:, i, :])
                ins.then_inc(router, 1)
                dve.wait_ge(router, r0 + 2)
                for i in range(a, b):
                    ins = dve.max_index(top_id[:, i, :], top[:, i, :], logits[:, i, :])
                ins.then_inc(router, 1)
                dve.tensor_tensor(gap[:, a:b], top[:, a:b, 0], top[:, a:b, 1], ALU.subtract).then_inc(router, 1)
                dve.wait_ge(router, r0 + 4)
                dve.tensor_copy(top_idf[:, a:b, :], top_id[:, a:b, 0:2]).then_inc(router, 1)
                dve.wait_ge(router, r0 + 5)
                for k in range(2):
                    ins = dve.tensor_tensor(pick[:, k, a:b, :],
                                            expert_ids[:].unsqueeze(1).broadcast_to([P, n, EXPERTS]),
                                            top_idf[:, a:b, k:k + 1].broadcast_to([P, n, EXPERTS]), ALU.is_equal)
                ins.then_inc(route_done, 1)
                dve.wait_ge(route_done, 3 * part + 1)
                dve.wait_ge(share_done, 2 * part + 2)
                for k in range(2):
                    ins = dve.tensor_tensor(pick[:, k, a:b, :], pick[:, k, a:b, :],
                                            share[:, k, a:b].unsqueeze(2).broadcast_to([P, n, EXPERTS]),
                                            ALU.mult)
                ins.then_inc(route_done, 1)
                dve.wait_ge(route_done, 3 * part + 2)
                dve.tensor_tensor(route[:, a:b, :], pick[:, 0, a:b, :], pick[:, 1, a:b, :], ALU.add)\
                    .then_inc(route_done, 1)

            def route_rests(part):
                a, b = PARTS[part]
                dve.wait_ge(route_hi_done, part + 1)
                dve.tensor_tensor(route_st[32:40, a * P:b * P], bank[ROUTER_BANK[part]][0:EXPERTS, 0:(b - a) * P],
                                  route_st[0:EXPERTS, a * P:b * P].bitcast(F32), ALU.subtract)\
                    .then_inc(route_lo_done, 1)

            def hidden(u):
                n = part_range(units[u][0])[1]
                r = u % RING
                dve.wait_ge(glu_done, u + 1)
                dve.wait_ge(up_done, u + 1)
                if u >= RING:
                    dve.wait_ge(hid_hi_done, u - RING + 1)
                    dve.wait_ge(hid_lo_done, u - RING + 1)
                dve.scalar_tensor_tensor(out=hid[:, r, 0:n], in0=up[:, r, 0:n], scalar=1.0 - LIMIT,
                                         in1=glu[:, r, 0:n], op0=ALU.max, op1=ALU.mult).then_inc(hid_done, 1)

            def hidden_lo(u):
                n = part_range(units[u][0])[1]
                r = u % RING
                dve.wait_ge(hid_hi_done, u + 1)
                if u >= RING:
                    dve.wait_ge(down_ps, tiles_down(u - RING))
                dve.tensor_tensor(hid_lo[:, r, 0:n], hid[:, r, 0:n], hid_hi[:, r, 0:n].bitcast(F32),
                                  ALU.subtract).then_inc(hid_lo_done, 1)

            def sum_stats(*tiles):
                for i in tiles:
                    rows = LAST if i == TILES - 1 else P
                    dve.wait_ge(down_ps, tiles_down(FT - 1) if i < 2 else tiles_down(UNITS - 1) - (i < 4))
                    dve.tensor_tensor(y2[0:rows, i, :], acc(i), h1[0:rows, i, :], ALU.add).then_inc(y2_done, 1)
                for i in tiles:
                    rows = LAST if i == TILES - 1 else P
                    dve.wait_ge(y2_done, i + 1)
                    dve.bn_stats(stats[0:rows, i, :], y2[0:rows, i, :]).then_inc(stats2_done, 1)
                for i in tiles:
                    rows = LAST if i == TILES - 1 else P
                    dve.wait_ge(stats2_done, i + 1)
                    dve.bn_aggr(mv[0:rows, i, :], stats[0:rows, i, :]).then_inc(mv2_done, 1)

            def results(lot, a, b):
                dve.wait_ge(std2_done, lot + 1)
                dve.reciprocal(rstd[:, a:b], std[:, a:b]).then_inc(rstd2_done, 1)
                dve.wait_ge(rstd2_done, lot + 1)
                for i in range(a, b):
                    rows = LAST if i == TILES - 1 else P
                    dve.tensor_scalar(result[0:rows, i, :], y2[0:rows, i, :], mv[0:rows, i, 0:1],
                                      rstd[0:rows, i:i + 1], ALU.subtract, ALU.mult).then_inc(result_done, 1)

            for u in range(UNITS + LO_LAG):
                if u < UNITS:
                    part, t = units[u]
                    n = part_range(part)[1]
                    r = u % RING
                    dve.wait_ge(gate_ps, u + 1)
                    if u >= RING:
                        dve.wait_ge(glu_done, u - RING + 1)
                    dve.tensor_scalar(gate[:, r, 0:n], bank[u % 2][:, 0:n],
                                      sm[:, COL["bg"][0] + t:COL["bg"][0] + t + 1], LIMIT, ALU.add, ALU.min)\
                        .then_inc(gate_done, 1)
                    dve.wait_ge(up_ps, u + 1)
                    if u >= RING:
                        dve.wait_ge(hid_done, u - RING + 1)
                    dve.tensor_scalar(up[:, r, 0:n], bank[2 + u % 2][:, 0:n], bu1[:, t:t + 1], LIMIT + 1.0,
                                      ALU.add, ALU.min).then_inc(up_done, 1)
                if u == 0:
                    choose(0)
                if u == 1:
                    h1_rests(1)
                    route_rests(0)
                if u == 2:
                    choose(1)
                if u == 3:
                    route_rests(1)
                if HIDDEN_LAG <= u < UNITS + HIDDEN_LAG:
                    hidden(u - HIDDEN_LAG)
                if u >= LO_LAG:
                    hidden_lo(u - LO_LAG)
                if u == FT + DOWN_LAG + 1:
                    sum_stats(0)
                if u == FT + DOWN_LAG + 2:
                    sum_stats(1)
            results(0, 0, 2)
            sum_stats(2, 3, 4)
            dve.wait_ge(mv2_done, TILES)
            results(1, 2, TILES)

        @block.tensor
        def _(pe):
            outs = [(0, 0, P, 0), (2, P, D, 0), (1, 0, P, 1), (3, P, D, 1)]
            for c in range(CHUNKS - 1):
                pe.wait_ge(we_lo_done, c + 1)
                terms = ((we_hi, x_hi, x_hi_done), (we_lo, x_hi, x_hi_done), (we_hi, x_lo, x_lo_done))
                for k, (w, x, ready) in enumerate(terms):
                    pe.wait_ge(ready, c + 1)
                    for b, d0, d1, half in outs:
                        mm = pe.matmul(bank[b][0:d1 - d0, 0:HALF], w[:, c, d0:d1],
                                       x[:, c % X_RING, half * HALF:(half + 1) * HALF],
                                       start=(c == 0 and k == 0), stop=False)
                mm.then_inc(emb_chunk, 1)
            c = CHUNKS - 1
            pe.wait_ge(we_lo_done, CHUNKS)
            pe.wait_ge(x_hi_done, CHUNKS)
            pe.wait_ge(x_lo_done, CHUNKS)
            for b, d0, d1, half in outs:
                for k, (w, x) in enumerate(((we_hi, x_hi), (we_lo, x_hi), (we_hi, x_lo))):
                    mm = pe.matmul(bank[b][0:d1 - d0, 0:HALF], w[:, c, d0:d1],
                                   x[:, c % X_RING, half * HALF:(half + 1) * HALF],
                                   start=False, stop=(k == 2))
                mm.then_inc(emb_done, 1)

            pe.wait_ge(wqk_lo_done, 4)
            pe.wait_ge(h_lo_done, 4)
            for n in range(2 * QG):
                g, w = n // 2, n % 2
                ps = bank[(4 + n) % 8][:, 0:HALF]
                mms = 0
                for m in range(MEMBERS):
                    wc = slice(DB - m * DB, DB - m * DB + P)
                    hc = slice(m * HALF, (m + 1) * HALF)
                    for wt, r, h in ((wqk_hi, 0, h_ahi), (wqk_lo, 0, h_ahi), (wqk_hi, 0, h_alo),
                                     (wqk_hi, 1, h_bst), (wqk_lo, 1, h_bst)):
                        mm = pe.matmul(ps, wt[:, w, r, g, wc], h[:, hc], start=(mms == 0), stop=(mms == 9))
                        mms += 1
                mm.then_inc(qk_ps, 1)

            def scores(p):
                ps = bank[6 + p % 2]
                if p == 0:
                    pe.wait_ge(prep_done, PREP + 2)
                    pe.wait_ge(q_done, 2 * QG)
                    pe.wait_ge(k_done, QG * QH)
                if p >= 2:
                    pe.wait_ge(shift_done, p - 1)
                pe.matmul(ps[0:PAIR_TOKENS, 0:SCORES].rearrange("q (h k) -> q h k", h=HEADS),
                          ident_bf[0:PAIR_TOKENS, 0:PAIR_TOKENS],
                          causal_bf[0:PAIR_TOKENS, :].unsqueeze(1).broadcast_to([PAIR_TOKENS, HEADS, SEQ]),
                          start=True, stop=False)
                for g in range(QG):
                    mm = pe.matmul(ps[0:PAIR_TOKENS, g * QH * SEQ:(g + 1) * QH * SEQ], queries[:, g, p, :],
                                   keys[:, g, p].rearrange("d h k -> d (h k)"), start=False, stop=(g == QG - 1))
                mm.then_inc(scores_ps, 1)

            def pair_values(p):
                if p == 0:
                    pe.wait_ge(rep_done, 3)
                    pe.wait_ge(wv_lo_done, 1)
                if p >= 2:
                    pe.wait_ge(v_done, p - 1)
                for m in range(MEMBERS):
                    terms = ((rep[0], wv_hi, 0), (rep[0], wv_lo, 0), (rep[1], wv_hi, 0),
                             (rep[2], wv_hi, 1), (rep[2], wv_lo, 1))
                    for k, (h, wt, r) in enumerate(terms):
                        mm = pe.matmul(bank[4 + p % 2][0:KEYS, m * D:(m + 1) * D],
                                       h[:, m * PAIRS + p].rearrange("d v k -> d (v k)"), wt[:, r, :],
                                       start=(k == 0), stop=(k == 4))
                mm.then_inc(v_ps, 1)

            def turn(p):
                pe.wait_ge(probs_done, p + 1)
                if p >= 2:
                    pe.wait_ge(probs_t_done, p - 1)
                for g in range(VG):
                    mm = pe.transpose(bank[p % 2][0:KEYS, g * PAIR_TOKENS:(g + 1) * PAIR_TOKENS],
                                      probs[:, p % 2, g * KEYS:(g + 1) * KEYS],
                                      sm[0:PAIR_TOKENS, COL["ident"][0]:COL["ident"][0] + PAIR_TOKENS])
                mm.then_inc(probs_ps, 1)

            def contexts(p):
                pe.wait_ge(probs_t_done, p + 1)
                pe.wait_ge(v_done, p + 1)
                if p >= 2:
                    pe.wait_ge(ctx_done, 2 * (p - 1))
                for m in range(MEMBERS):
                    for g in range(VG):
                        r0, c0 = VW * (g % 2), (g // 2) * PAIR_TOKENS + m * SEQ
                        mm = pe.matmul(bank[2 + p % 2][r0:r0 + VW, c0:c0 + SEQ], values[:, m, p, g, :],
                                       probs_t[:, p % 2, g, m * SEQ:(m + 1) * SEQ], start=True, stop=True)
                mm.then_inc(ctx_ps, 1)

            ident = col("ident")

            def project(i):
                cols = slice(i * P, (i + 1) * P)
                y = bank[Y_BANK[i]]
                pe.matmul(y[:, 0:D], ctx_t[:, 0, cols], wo_sb[:, 0, :], start=True, stop=False)
                pe.matmul(y[:, 0:D], ctx_t[:, 1, cols], wo_sb[:, 1, :], start=False, stop=False)
                pe.matmul(y[:, 0:P], res_a[:, cols], ident, start=False, stop=False)
                pe.matmul(y[:, P:D], res_b[:, cols], ident[0:DB, 0:DB], start=False, stop=True)\
                    .then_inc(y_ps, 1)

            for p in range(PAIRS + 3):
                if p < PAIRS:
                    scores(p)
                if 1 <= p <= PAIRS:
                    pair_values(p - 1)
                if 2 <= p < PAIRS + 2:
                    turn(p - 2)
                if p >= 3:
                    contexts(p - 3)
                if p == PAIRS:
                    pe.wait_ge(wo_in, 16)
                    pe.wait_ge(ctx_done, 2 * 2)
                    pe.wait_ge(shift_done, PAIRS - 1)
                    project(0)
                if p == PAIRS + 1:
                    pe.wait_ge(ctx_done, 2 * 4)
                    pe.wait_ge(v_done, PAIRS - 1)
                    project(1)
                    pe.wait_ge(ctx_done, 2 * 6)
                    pe.wait_ge(shift_done, PAIRS)
                    project(2)
                if p == PAIRS + 2:
                    pe.wait_ge(ctx_done, 2 * 7)
                    pe.wait_ge(v_done, PAIRS)
                    project(3)

            def turn_h1(part):
                a, b = PARTS[part]
                for r, (c0, c1) in enumerate(((0, P), (P, D))):
                    for i in range(a, b):
                        pe.wait_ge(h1_done, i + 1)
                        mm = pe.transpose(bank[H1T_BANK[part][r]][0:c1 - c0, (i - a) * P:(i - a + 1) * P],
                                          h1[:, i, c0:c1], ident)
                    mm.then_inc(h1t_ps, 1)

            turn_h1(0)
            pe.wait_ge(ctx_done, 2 * PAIRS)
            project(4)

            def router_logits(part):
                a, b = PARTS[part]
                pe.wait_ge(h1_hi_done, 2 * part + 2)
                pe.wait_ge(h1_lo_done, 2 * part + 2)
                if part == 0:
                    pe.wait_ge(h1_done, 3)
                for i in range(a, b):
                    cols = slice(i * P, (i + 1) * P)
                    terms = ((h1_ahi, wr_hi, 0), (h1_alo, wr_hi, 0), (h1_ahi, wr_lo, 0),
                             (h1_bst, wr_hi, 1), (h1_bst, wr_lo, 1))
                    for k, (h, wt, r) in enumerate(terms):
                        mm = pe.matmul(bank[ROUTER_BANK[part]][:, (i - a) * EXPERTS:(i - a + 1) * EXPERTS],
                                       h[:, cols], wt[:, r * EXPERTS:(r + 1) * EXPERTS],
                                       start=(k == 0), stop=(k == 4))
                mm.then_inc(logit_ps, 1)

            def gate_up(u):
                part, t = units[u]
                t0, n = part_range(part)
                lot = t // TL
                if t == 0:
                    pe.wait_ge(h1_lo_done, 2 * part + 2)
                if part == 0 and t % TL == 0:
                    pe.wait_ge(split_done, 2 * lot + 2)
                for which, done, used in ((0, gate_ps, gate_done), (1, up_ps, up_done)):
                    if u >= 2:
                        pe.wait_ge(used, u - 1)
                    ps = bank[2 * which + u % 2][:, 0:n]
                    wa, wb = expert_weights(t, which)
                    terms = ((experts_hi, wa, h1_ahi), (experts_lo, wa, h1_ahi), (experts_hi, wa, h1_alo),
                             (experts_hi, wb, h1_bst), (experts_lo, wb, h1_bst))
                    for k, (wt, w, h) in enumerate(terms):
                        mm = pe.matmul(ps, wt[:, lot, w], h[:, t0:t0 + n], start=(k == 0), stop=(k == 4))
                    mm.then_inc(done, 1)

            def routes(part):
                a, b = PARTS[part]
                pe.wait_ge(route_done, 3 * part + 3)
                for i in range(a, b):
                    mm = pe.transpose(bank[ROUTER_BANK[part]][0:EXPERTS, (i - a) * P:(i - a + 1) * P],
                                      route[:, i, :], ident)
                mm.then_inc(route_ps, 1)

            def spreads(u):
                part, t = units[u]
                t0, n = part_range(part)
                if t == 0:
                    pe.wait_ge(route_lo_done, part + 1)
                if u >= 1:
                    pe.wait_ge(spread_done, u)
                pe.matmul(bank[6][:, 0:n], sel_sb[:, t * P:(t + 1) * P], route_st[:, t0:t0 + n],
                          start=True, stop=True).then_inc(spread_ps, 1)

            def down(u):
                part, t = units[u]
                a, b = PARTS[part]
                pe.wait_ge(hid_lo_done, u + 1)
                if t == 0:
                    for i in range(a, b):
                        rows = LAST if i == TILES - 1 else P
                        for k, wt in enumerate((bd_hi, bd_lo)):
                            pe.matmul(acc(i), route_st[:, i * P:i * P + rows], wt[:],
                                      start=(k == 0 and i % 2 == 0), stop=False, skip_group_check=True)
                for i in range(a, b):
                    rows = LAST if i == TILES - 1 else P
                    cols = slice((i - a) * P, (i - a) * P + rows)
                    for k, (h, wt) in enumerate(((hid_hi, experts_hi), (hid_lo, experts_hi),
                                                 (hid_hi, experts_lo))):
                        mm = pe.matmul(acc(i), h[:, u % RING, cols], wt[:, t // TL, down_weights(t)],
                                       start=False, stop=(t == FT - 1 and k == 2), skip_group_check=True)
                    mm.then_inc(down_ps, 1)

            pe.wait_ge(sel_done, 1)
            for u in range(UNITS + DOWN_LAG):
                if u < UNITS:
                    gate_up(u)
                if u == 0:
                    router_logits(0)
                if u == 1:
                    turn_h1(1)
                    routes(0)
                if u == 2:
                    router_logits(1)
                if u == 3:
                    routes(1)
                if SPREAD_LAG <= u < UNITS + SPREAD_LAG:
                    spreads(u - SPREAD_LAG)
                if u >= DOWN_LAG:
                    down(u - DOWN_LAG)


_OUTS = [((TOKENS, D), "float32")]


def kernel(**inputs):
    import numpy as np
    import concourse.bacc as bacc
    from concourse.bass_utils import run_bass_kernel_spmd

    x = np.asarray(inputs["x"])
    f = {k: np.asarray(v) for k, v in inputs.items()}
    side = 6
    px = 16

    patches = x.reshape(IMAGES, 3, side, px, side, px).transpose(0, 2, 4, 1, 3, 5)
    patches = patches.reshape(IMAGES, SEQ - 1, PATCH_DIM)
    patches = np.pad(patches, ((0, 0), (1, 0), (0, 0))).reshape(TOKENS, PATCH_DIM)
    x_t = patches.T.reshape(CHUNKS, P, TOKENS).transpose(1, 0, 2)
    w_emb = f["L0_tok_W_emb"].reshape(CHUNKS, P, D).transpose(1, 0, 2)

    def a_b(w):
        return np.stack([w[:P], np.concatenate([w[P:], w[P:]])], axis=1)

    def flat(w):
        return w.transpose(1, 0, 2).reshape(D, HEADS * HD)

    w_qk = np.stack([a_b(flat(f["L0_attn_Wq"])), a_b(flat(f["L0_attn_Wk"]))], axis=1)
    w_v = a_b(flat(f["L0_attn_Wv"]))
    wo = np.zeros((P, 2, D), np.float32)
    bv = np.zeros((P, 2), np.float32)
    bv_flat = f["L0_attn_bv"].reshape(-1)
    used = VH * HD
    for g in range(VG):
        r0 = VW * (g % 2)
        wo[r0:r0 + used, g // 2] = f["L0_attn_Wo"][g * used:(g + 1) * used]
        bv[r0:r0 + used, g // 2] = bv_flat[g * used:(g + 1) * used]
    wo[used, 0] = f["L0_attn_bo"]
    bv[used, 0] = 1.0

    small = np.zeros((P, SMALL), np.float32)

    def put(name, a):
        c0, c1 = COL[name]
        small[:a.shape[0], c0:c1] = a.reshape(a.shape[0], -1)

    pos = f["L0_tok_pos_embedding"][0, :SEQ].T
    for part, rows in (("a", slice(0, P)), ("b", slice(P, D))):
        put(f"pos_{part}", pos[rows])
        put(f"bemb_{part}", f["L0_tok_b_emb"][rows][:, None])
        put(f"cls_{part}", f["L0_tok_cls_token"].reshape(-1)[rows][:, None])
    for name, b in (("bq", f["L0_attn_bq"]), ("bk", f["L0_attn_bk"])):
        t = b.reshape(QG, QH * HD).T
        put(name, np.concatenate([t, t]))
    put("bv", bv)
    put("bg", f["L0_ffn_bgu"][:, :INNER].reshape(FT, P).T)
    put("bu", f["L0_ffn_bgu"][:, INNER:].reshape(FT, P).T)
    put("br", np.broadcast_to(f["L0_ffn_br"], (P, EXPERTS)))
    wr = a_b(f["L0_ffn_Wr"])
    put("wr_a", wr[:, 0])
    put("wr_b", wr[:, 1])
    rows = np.arange(P)
    put("head_mask", (rows[:, None] % DB // HD == np.arange(QH)).astype(np.float32))
    keys = np.arange(KEYS)
    put("value_mask", (keys[:, None] // SEQ == np.arange(VH * HD) // HD).astype(np.float32))
    queries = np.arange(PAIR_TOKENS) % SEQ
    put("causal", np.where(np.arange(SEQ) > queries[:, None], MASKED, 0.0).astype(np.float32))
    put("ident", np.eye(P, dtype=np.float32))
    bd = np.zeros((40, D), np.float32)
    bd[0:EXPERTS] = f["L0_ffn_bd"]
    bd[32:40] = f["L0_ffn_bd"]
    put("bd", bd)

    owner = np.arange(EXPERTS * INNER) // INNER
    sel = np.zeros((40, FT * P), np.float32)
    sel[owner, np.arange(FT * P)] = 1.0
    sel[32 + owner, np.arange(FT * P)] = 1.0

    wgu = f["L0_ffn_Wgu"].transpose(1, 0, 2)
    g_ab = a_b(wgu[:, :, :INNER].reshape(D, FT * P))
    u_ab = a_b(wgu[:, :, INNER:].reshape(D, FT * P))
    w_d = f["L0_ffn_Wd"].reshape(FT, P, D).transpose(1, 0, 2)

    def lots(w):
        return w.reshape(P, LOTS, -1)

    w_experts = np.concatenate([lots(g_ab[:, 0]), lots(u_ab[:, 0]), lots(g_ab[:, 1]), lots(u_ab[:, 1]),
                                lots(w_d)], axis=2)

    nc = bacc.Bacc("TRN2", target_bir_lowering=False, num_devices=1)
    arrays, args = {}, []
    for name, a in (("x_t", x_t), ("w_emb", w_emb), ("small", small), ("w_qk", w_qk), ("w_v", w_v),
                    ("w_o", wo), ("sel", sel), ("w_experts", w_experts)):
        arrays[name] = np.ascontiguousarray(a)
        args.append(nc.dram_tensor(name, a.shape, mybir.dt.from_np(a.dtype), kind="ExternalInput").ap())
    args.append(nc.dram_tensor("out_0", (TOKENS, D), F32, kind="ExternalOutput").ap())
    build_program(nc, *args)
    r = run_bass_kernel_spmd(nc, [arrays], core_ids=[0])
    return r.results[0]["out_0"].reshape(IMAGES, SEQ, D)
```

```python
from contextlib import ExitStack

import concourse.bass as bass
from concourse import mybir

F32 = mybir.dt.float32
F32R = mybir.dt.float32r
BF16 = mybir.dt.bfloat16
U32 = mybir.dt.uint32
ALU = mybir.AluOpType
ACT = mybir.ActivationFunctionType
AX_X = mybir.AxisListType.X

P = 128
IMAGES, SEQ, D = 16, 37, 192
TOKENS = IMAGES * SEQ
HALF = TOKENS // 2
DB = D - P
PATCH_DIM = 768
CHUNKS = PATCH_DIM // P
HEADS, HD = 12, 16
PAIRS, MEMBERS = IMAGES // 2, 2
QG = 3
QH = HEADS // QG
VG = 4
VH = HEADS // VG
VW = 64
PAIR_TOKENS = MEMBERS * SEQ
SCORES = HEADS * SEQ
KEYS = VH * SEQ
EXPERTS, INNER = 8, 192
FT = EXPERTS * INNER // P
TILES = 5
PADDED = TILES * P
LAST = TOKENS - (TILES - 1) * P
PARTS = [(0, 2), (2, 5)]
X_RING = 4
LOTS = 6
TL = FT // LOTS
LOT_GU = TL * P
LOT = 4 * LOT_GU + TL * D
PIECES = 2 * LOTS
PIECE = LOT // 2
STAGES = 4
ATT_SCALE = 0.25
ALPHA, LIMIT, EPS = 1.702, 7.0, 1e-5
MASKED = -1e37

_COLS = [("pos_a", SEQ), ("pos_b", SEQ), ("bemb_a", 1), ("bemb_b", 1), ("cls_a", 1), ("cls_b", 1),
         ("bq", QG), ("bk", QG), ("bv", 2), ("bg", FT), ("bu", FT), ("br", EXPERTS),
         ("wr_a", EXPERTS), ("wr_b", EXPERTS), ("head_mask", QH), ("value_mask", VH * HD),
         ("causal", SEQ), ("ident", P), ("bd", D)]
COL = {}
_at = 0
for _name, _n in _COLS:
    COL[_name] = (_at, _at + _n)
    _at += _n
SMALL = _at


def part_range(part):
    a, b = PARTS[part]
    return a * P, min(b * P, TOKENS) - a * P


def build_program(nc, x_t, w_emb, small, w_qk, w_v, w_o, sel, w_experts, out):
    with ExitStack() as ctx:
        def sb(stack, name, shape, dt=F32):
            return stack.enter_context(nc.sbuf_tensor(name, shape, dt))

        def sem(name):
            return ctx.enter_context(nc.semaphore(name))

        sm = sb(ctx, "sm", [P, SMALL])
        ident_bf = sb(ctx, "ident_bf", [P, P], BF16)
        causal_bf = sb(ctx, "causal_bf", [P, SEQ], BF16)
        bu1 = sb(ctx, "bu1", [P, FT])
        eps = sb(ctx, "eps", [P, 1])
        expert_ids = sb(ctx, "expert_ids", [P, EXPERTS])
        wr_sb = sb(ctx, "wr_sb", [P, 2, 2, EXPERTS], F32R)
        bd_hi = sb(ctx, "bd_hi", [40, D], F32R)
        bd_lo = sb(ctx, "bd_lo", [40, D], F32R)
        res_a = sb(ctx, "res_a", [P, PADDED])
        res_b = sb(ctx, "res_b", [DB, PADDED])
        wo_sb = sb(ctx, "wo_sb", [P, 2, D])
        h1 = sb(ctx, "h1", [P, TILES, D])
        h1_ahi = sb(ctx, "h1_ahi", [P, PADDED], F32R)
        h1_alo = sb(ctx, "h1_alo", [P, PADDED], F32R)
        h1_bst = sb(ctx, "h1_bst", [P, PADDED], F32R)
        stats = sb(ctx, "stats", [P, TILES, 6])
        mv = sb(ctx, "mv", [P, TILES, 2])
        std = sb(ctx, "std", [P, TILES])
        rstd = sb(ctx, "rstd", [P, TILES])
        logits = sb(ctx, "logits", [P, TILES, EXPERTS])
        top = sb(ctx, "top", [P, TILES, EXPERTS])
        top_id = sb(ctx, "top_id", [P, TILES, EXPERTS], U32)
        top_idf = sb(ctx, "top_idf", [P, TILES, 2])
        gap = sb(ctx, "gap", [P, TILES])
        share = sb(ctx, "share", [P, 2, TILES])
        pick = sb(ctx, "pick", [P, 2, TILES, EXPERTS])
        route = sb(ctx, "route", [P, TILES, EXPERTS])
        route_st = sb(ctx, "route_st", [40, PADDED], F32R)
        sel_sb = sb(ctx, "sel_sb", [40, FT * P], F32R)
        warm = sb(ctx, "warm", [P, 1])
        shift2 = sb(ctx, "shift2", [P, 1])
        zeros_bf = sb(ctx, "zeros_bf", [P, 512], BF16)
        stage = sb(ctx, "stage", [P, STAGES, PIECE])

        with ExitStack() as early:
            x_hi = sb(early, "x_hi", [P, X_RING, TOKENS], F32R)
            x_lo = sb(early, "x_lo", [P, X_RING, TOKENS], F32R)
            x_raw = sb(early, "x_raw", [P, CHUNKS, TOKENS])
            we_raw = sb(early, "we_raw", [P, CHUNKS, D])
            we_sb = sb(early, "we_sb", [P, CHUNKS, 2 * D], F32R)
            sel_raw = sb(early, "sel_raw", [40, FT * P])
            wqk_raw = sb(early, "wqk_raw", [P, 2, 2, D])
            wv_raw = sb(early, "wv_raw", [P, 2, D])
        experts_hi = sb(ctx, "experts_hi", [P, LOTS, LOT], F32R)
        experts_lo = sb(ctx, "experts_lo", [P, LOTS, LOT], F32R)
        ctx_t = sb(ctx, "ctx_t", [P, 2, PADDED])

        with ExitStack() as att:
            keys = sb(att, "keys", [P, QG, PAIRS, QH, SEQ])
            values = sb(att, "values", [KEYS, MEMBERS, PAIRS, VG, VW])
            queries = sb(att, "queries", [P, QG, PAIRS, PAIR_TOKENS])
            rep = [sb(att, f"rep_{n}", [P, IMAGES, VH, SEQ], F32R) for n in ("ahi", "alo", "bst")]
            wv_hi = sb(att, "wv_hi", [P, 2, D], F32R)
            wv_lo = sb(att, "wv_lo", [P, 2, D], F32R)
            with ExitStack() as proj:
                wqk_hi = sb(proj, "wqk_hi", [P, 2, 2, QG, 3 * DB], F32R)
                wqk_lo = sb(proj, "wqk_lo", [P, 2, 2, QG, 3 * DB], F32R)
                h_ahi = sb(proj, "h_ahi", [P, TOKENS], F32R)
                h_alo = sb(proj, "h_alo", [P, TOKENS], F32R)
                h_bst = sb(proj, "h_bst", [P, TOKENS], F32R)
                all_keys = sb(proj, "all_keys", [P, 2, PAIRS, SEQ])
            shifted = sb(att, "shifted", [PAIR_TOKENS, 2, SCORES])
            expd = sb(att, "expd", [PAIR_TOKENS, 2, SCORES])
            probs = sb(att, "probs", [PAIR_TOKENS, 2, SCORES])
            probs_t = sb(att, "probs_t", [KEYS, 2, VG, PAIR_TOKENS])
            top_score = sb(att, "top_score", [PAIR_TOKENS, 2, HEADS])
            prob_sum = sb(att, "prob_sum", [PAIR_TOKENS, 2, HEADS])
            prob_inv = sb(att, "prob_inv", [PAIR_TOKENS, 2, HEADS])
            NMAX = part_range(1)[1]
            GU_RING, RING = 5, 5
            gate = sb(att, "gate", [P, GU_RING, NMAX])
            up = sb(att, "up", [P, GU_RING, NMAX])
        sig = sb(ctx, "sig", [P, RING, NMAX])
        spread = sb(ctx, "spread", [P, RING, NMAX])
        sig_w = sb(ctx, "sig_w", [P, RING, NMAX])
        glu = sb(ctx, "glu", [P, RING, NMAX])
        hid = sb(ctx, "hid", [P, RING, NMAX])
        hid_hi = sb(ctx, "hid_hi", [P, RING, NMAX], F32R)
        hid_lo = sb(ctx, "hid_lo", [P, RING, NMAX], F32R)
        y2 = sb(ctx, "y2", [P, 2, D])
        result = sb(ctx, "result", [P, TILES, D])

        bank = [ctx.enter_context(nc.psum_tensor(f"bank{i}", [P, 512], F32)) for i in range(8)]

        x_in = [sem(f"x_in{c}") for c in range(CHUNKS)]
        we_first_in, we_in, small_in, wqk_in, wv_in, wo_in, sel_in = (
            sem(n) for n in ("we_first_in", "we_in", "small_in", "wqk_in", "wv_in", "wo_in", "sel_in"))
        stage_in = [sem(f"stage_in{i}") for i in range(PIECES)]
        out_done = [sem(f"out_done{i}") for i in range(3)]
        shift2_done, last_done = sem("shift2_done"), sem("last_done")
        warm_done = sem("warm_done")
        zeros_done = sem("zeros_done")
        zero_fill = sem("zero_fill")
        pool_zero = sem("pool_zero")
        prep_done = sem("prep_done")
        x_hi_done, x_lo_done = sem("x_hi_done"), sem("x_lo_done")
        we_hi_done, we_lo_done = sem("we_hi_done"), sem("we_lo_done")
        emb_chunk, emb_done = sem("emb_chunk"), sem("emb_done")
        res_b_part, res_done, h_hi_done, h_lo_done = sem("res_b_part"), sem("res_done"), sem("h_hi_done"), sem("h_lo_done")
        wqk_hi_done, wqk_lo_done = sem("wqk_hi_done"), sem("wqk_lo_done")
        qk_ps, q_done, k_done, all_keys_done = (sem(n) for n in ("qk_ps", "q_done", "k_done", "all_keys_done"))
        rep_done, v_ps, v_done = sem("rep_done"), sem("v_ps"), sem("v_done")
        scores_ps, top_done, shift_done, exp_done = (
            sem(n) for n in ("scores_ps", "top_done", "shift_done", "exp_done"))
        sum_done, inv_done, probs_done = sem("sum_done"), sem("inv_done"), sem("probs_done")
        probs_ps, probs_t_done, ctx_ps, ctx_done = (
            sem(n) for n in ("probs_ps", "probs_t_done", "ctx_ps", "ctx_done"))
        y_ps, stats_done, mv_done, std_done, rstd_done, h1_done = (
            sem(n) for n in ("y_ps", "stats_done", "mv_done", "std_done", "rstd_done", "h1_done"))
        h1t_ps, h1_hi_done, h1_lo_done = sem("h1t_ps"), sem("h1_hi_done"), sem("h1_lo_done")
        logit_ps, router, share_done, route_done = (
            sem(n) for n in ("logit_ps", "router", "share_done", "route_done"))
        route_ps, route_hi_done, route_lo_done = (
            sem(n) for n in ("route_ps", "route_hi_done", "route_lo_done"))
        split_hi, split_done = sem("split_hi"), sem("split_done")
        wv_hi_done, wv_lo_done, sel_done = sem("wv_hi_done"), sem("wv_lo_done"), sem("sel_done")
        spread_ps, gate_ps, up_ps = sem("spread_ps"), sem("gate_ps"), sem("up_ps")
        spread_done, gate_done, up_done, sig_done = (
            sem(n) for n in ("spread_done", "gate_done", "up_done", "sig_done"))
        sigw_done, glu_done, hid_done = sem("sigw_done"), sem("glu_done"), sem("hid_done")
        hid_hi_done, hid_lo_done, down_ps = sem("hid_hi_done"), sem("hid_lo_done"), sem("down_ps")
        y2_done, stats2_done, mv2_done, std2_done, rstd2_done, result_done = (
            sem(n) for n in ("y2_done", "stats2_done", "mv2_done", "std2_done", "rstd2_done", "result_done"))

        def col(name, rows=P):
            a, b = COL[name]
            return sm[0:rows, a:b]

        units = [(part, t) for part in range(2) for t in range(FT)]
        UNITS = len(units)
        SPREAD = (2, 2, (8, 16))
        HIDDEN = (4, 4, (8, 13, 18))
        LO = (5, 5, (9, 14, 19))
        DOWN = (6, 6, (10, 15, 20))

        def due(u, step):
            lag, first, sooner = step

            def upto(v):
                return min(UNITS, v + 1 - lag + sum(v >= c for c in sooner)) if v >= first else 0
            return range(upto(u - 1), upto(u))

        GLU_ON_DVE = 2
        LAST_STEP = UNITS + DOWN[0] - len(DOWN[2])
        FIRST_PART_DOWN = next(u for u in range(LAST_STEP) if FT - 1 in due(u, DOWN))

        def tiles_down(u):
            return sum(PARTS[part][1] - PARTS[part][0] for part, _ in units[:u + 1])

        def acc(i):
            rows = LAST if i == TILES - 1 else P
            j = i if i < 2 else 0
            return bank[DOWN_BANK[i]][0:rows, j * D:(j + 1) * D]

        def expert_weights(t, half):
            at = (t % TL) * P
            return [slice((2 * r + half) * LOT_GU + at, (2 * r + half) * LOT_GU + at + P) for r in range(2)]

        def down_weights(t):
            at = 4 * LOT_GU + (t % TL) * D
            return slice(at, at + D)

        QK_BANK = (5, 6, 7, 4, 0, 1)
        SCORES_BANK, VALUES_BANK, PROBS_BANK, CTX_BANK = (6, 7), (4, 2), 5, 3
        Y_BANK = (0, 1, 7, 5, 3)
        H1T_BANK = ((2, 0), (5, 7))
        ROUTER_BANK = (4, 5)
        GATE_BANK, UP_BANK = (0, 2), (1, 6)
        DOWN_BANK = (4, 4, 5, 7, 4)

        def spread_bank(u):
            return 7 if 3 <= u < FT and u % 2 else 3

        WARM_UP = 9
        POSITIONS = 16
        PREP = 21

        def slots(t, half):
            return t.rearrange("d (m p k) -> d p m k", m=MEMBERS, p=PAIRS)[:, 4 * half:4 * half + 4]

        def qk_bank(g, w):
            return bank[QK_BANK[2 * g + 1 - w]][:, 0:HALF].rearrange("d (p k) -> d p k", p=PAIRS)

        def by_pair(t):
            return t.rearrange("d (p m k) -> d p m k", p=PAIRS // 2, m=MEMBERS)

        block = ctx.enter_context(nc.Block())

        @block.sync
        def _(sp):
            sp.dma_start(we_raw[:, 0, :], w_emb[:, 0, :]).then_inc(we_first_in, 16)
            for c in range(CHUNKS):
                sp.dma_start(x_raw[:, c, :], x_t[:, c, :]).then_inc(x_in[c], 16)
                if c == 0:
                    sp.dma_start(we_raw[:, 1:, :], w_emb[:, 1:, :]).then_inc(we_in, 16)
            sp.dma_start(wqk_raw[:], w_qk).then_inc(wqk_in, 16)
            sp.dma_start(sm[:], small).then_inc(small_in, 16)
            sp.dma_start(wv_raw[:], w_v).then_inc(wv_in, 16)
            sp.dma_start(sel_raw[:], sel).then_inc(sel_in, 16)
            for k in range(PIECES):
                if k >= STAGES:
                    sp.wait_ge(split_done, k - STAGES + 1)
                sp.dma_start(stage[:, k % STAGES, :], w_experts[:, k // 2, k % 2 * PIECE:(k % 2 + 1) * PIECE])\
                    .then_inc(stage_in[k], 16)
                if k == STAGES - 1:
                    sp.dma_start(wo_sb[:], w_o).then_inc(wo_in, 16)
            def store(n, a, b):
                sp.dma_start(out[a * P:b * P, :].rearrange("(i t) d -> t i d", t=P), result[:, a:b, :])\
                    .then_inc(out_done[n], 16)

            sp.wait_ge(result_done, 2)
            store(0, 0, 2)
            sp.wait_ge(last_done, 1)
            sp.dma_start(out[(TILES - 1) * P:TOKENS, :], result[0:LAST, TILES - 1, :]).then_inc(out_done[1], 16)
            sp.wait_ge(result_done, 4)
            store(2, 2, 4)
            for n in range(3):
                sp.wait_ge(out_done[n], 16)

        @block.gpsimd
        def _(pool):
            pool.memset(wqk_hi[:].bitcast(F32), 0.0).then_inc(pool_zero, 1)
            for c in range(CHUNKS):
                pool.wait_ge(we_first_in if c == 0 else we_in, 16)
                pool.tensor_scalar(we_sb[:, c, 0:D], we_raw[:, c, :], 1.0, 1.0, ALU.mult, ALU.mult)\
                    .then_inc(we_hi_done, 1)
                pool.wait_ge(we_hi_done, c + 1)
                pool.tensor_tensor(we_sb[:, c, 2 * P:3 * P], we_raw[:, c, 0:P], we_sb[:, c, 0:P].bitcast(F32),
                                   ALU.subtract).then_inc(we_lo_done, 1)
                pool.tensor_tensor(we_sb[:, c, D:2 * P], we_raw[:, c, P:D], we_sb[:, c, P:D].bitcast(F32),
                                   ALU.subtract).then_inc(we_lo_done, 1)
            pool.wait_ge(wqk_in, 16)
            pool.wait_ge(pool_zero, 1)
            pool.wait_ge(zero_fill, 1)
            for r in range(2):
                for w in range(2):
                    dst = wqk_hi[:, w, r, :, DB:2 * DB]
                    src = wqk_raw[:, w, r, :].rearrange("p (g c) -> p g c", g=QG)
                    pool.tensor_scalar(dst, src, 1.0, 1.0, ALU.mult, ALU.mult).then_inc(wqk_hi_done, 1)
                    pool.wait_ge(wqk_hi_done, 2 * r + w + 1)
                    pool.tensor_tensor(wqk_lo[:, w, r, :, DB:2 * DB], src, dst.bitcast(F32),
                                       ALU.subtract).then_inc(wqk_lo_done, 1)
            pool.memset(queries[:], 0.0).then_inc(pool_zero, 1)
            needs = ((2, 0), (2, 2), (4, 4))
            for dst, src, (hi, lo) in zip(rep, (h_ahi, h_alo, h_bst), needs):
                pool.wait_ge(h_hi_done, hi)
                if lo:
                    pool.wait_ge(h_lo_done, lo)
                view = src[:].bitcast(F32).rearrange("d (s k) -> d s k", s=IMAGES)
                pool.tensor_scalar(dst[:], view.unsqueeze(2).broadcast_to([P, IMAGES, VH, SEQ]), 1.0, 1.0,
                                   ALU.mult, ALU.mult).then_inc(rep_done, 1)
            pool.wait_ge(sel_in, 16)
            pool.tensor_scalar(sel_sb[:], sel_raw[:], 1.0, 1.0, ALU.mult, ALU.mult).then_inc(sel_done, 1)
            pool.memset(ctx_t[:, :, TOKENS:PADDED], 0.0).then_inc(pool_zero, 1)
            pool.wait_ge(emb_done, 4)
            pool.wait_ge(wqk_lo_done, 4)
            pool.wait_ge(wv_lo_done, 1)
            pool.wait_ge(sel_done, 1)

            def split_lo(k):
                lot, cols = k // 2, slice(k % 2 * PIECE, (k % 2 + 1) * PIECE)
                pool.wait_ge(split_hi, k + 1)
                pool.tensor_tensor(experts_lo[:, lot, cols], stage[:, k % STAGES, :],
                                   experts_hi[:, lot, cols].bitcast(F32), ALU.subtract).then_inc(split_done, 1)

            split_lo(0)
            split_lo(1)
            for p in range(PAIRS):
                pool.wait_ge(exp_done, p + 1)
                pool.wait_ge(inv_done, p + 1)
                if p >= 2:
                    pool.wait_ge(probs_ps, p - 1)
                pool.tensor_tensor(
                    probs[:, p % 2, :].rearrange("q (h k) -> q h k", h=HEADS),
                    expd[:, p % 2, :].rearrange("q (h k) -> q h k", h=HEADS),
                    prob_inv[:, p % 2, :].unsqueeze(2).broadcast_to([PAIR_TOKENS, HEADS, SEQ]),
                    ALU.mult).then_inc(probs_done, 1)
                if p < PAIRS - 2:
                    split_lo(p + 2)
            for k in range(PAIRS, PIECES):
                split_lo(k)
            for u, (part, t) in enumerate(units):
                n = part_range(part)[1]
                r = u % RING
                pool.wait_ge(sig_done, u + 1)
                pool.wait_ge(spread_done, u + 1)
                if u >= RING:
                    pool.wait_ge(glu_done, u - RING + 1)
                pool.tensor_tensor(sig_w[:, r, 0:n], sig[:, r, 0:n], spread[:, r, 0:n], ALU.mult)\
                    .then_inc(sigw_done, 1)
                if u >= UNITS - GLU_ON_DVE:
                    continue
                pool.wait_ge(sigw_done, u + 1)
                if u >= RING:
                    pool.wait_ge(hid_done, u - RING + 1)
                pool.tensor_tensor(glu[:, r, 0:n], sig_w[:, r, 0:n], gate[:, u % GU_RING, 0:n], ALU.mult)\
                    .then_inc(glu_done, 1)

        @block.scalar
        def _(act):
            def deviations(*tiles):
                for i in tiles:
                    act.wait_ge(mv_done, i + 1)
                    act.activation(std[:, i:i + 1], mv[:, i, 1:2], ACT.Sqrt, bias=eps[:]).then_inc(std_done, 1)

            def h1_rounded(part):
                c0 = PARTS[part][0] * P
                n = (PARTS[part][1] - PARTS[part][0]) * P
                bank_a, bank_b = H1T_BANK[part]
                act.wait_ge(h1t_ps, 2 * part + 1)
                act.activation(h1_ahi[:, c0:c0 + n], bank[bank_a][:, 0:n], ACT.Copy).then_inc(h1_hi_done, 1)
                act.wait_ge(h1t_ps, 2 * part + 2)
                act.activation(h1_bst[0:DB, c0:c0 + n], bank[bank_b][0:DB, 0:n], ACT.Copy)\
                    .then_inc(h1_hi_done, 1)

            def shares(part):
                a, b = PARTS[part]
                act.wait_ge(router, 6 * part + 5)
                for k, sign in ((0, 1.0), (1, -1.0)):
                    act.activation(share[:, k, a:b], gap[:, a:b], ACT.Sigmoid, scale=sign).then_inc(share_done, 1)

            def route_rounded(part):
                a, b = PARTS[part]
                act.wait_ge(route_ps, part + 1)
                act.activation(route_st[0:EXPERTS, a * P:b * P],
                               bank[ROUTER_BANK[part]][0:EXPERTS, 0:(b - a) * P],
                               ACT.Copy).then_inc(route_hi_done, 1)

            act.wait_ge(prep_done, 1)
            act.activation(warm[:], eps[:], ACT.Exp).then_inc(warm_done, 1)
            for c in range(CHUNKS):
                act.wait_ge(x_in[c], 16)
                if c >= X_RING:
                    act.wait_ge(emb_chunk, c - X_RING + 1)
                act.activation(x_hi[:, c % X_RING, :], x_raw[:, c, :], ACT.Copy).then_inc(x_hi_done, 1)
            act.wait_ge(wv_in, 16)
            act.activation(wv_hi[:], wv_raw[:], ACT.Copy).then_inc(wv_hi_done, 1)
            for n in range(4):
                half, res, dst = n % 2, (res_a, res_b)[n // 2], (h_ahi[:], h_bst[0:DB, :])[n // 2]
                cols = slice(half * HALF, (half + 1) * HALF)
                act.wait_ge(res_done, n + 1)
                act.activation(slots(dst, half), by_pair(res[:, cols]), ACT.Copy).then_inc(h_hi_done, 1)

            def split_hi_piece(k):
                lot, cols = k // 2, slice(k % 2 * PIECE, (k % 2 + 1) * PIECE)
                act.wait_ge(stage_in[k], 16)
                act.activation(experts_hi[:, lot, cols], stage[:, k % STAGES, :], ACT.Copy).then_inc(split_hi, 1)

            act.wait_ge(emb_done, 4)
            split_hi_piece(0)
            split_hi_piece(1)
            act.wait_ge(pool_zero, 2)
            for g in range(QG):
                act.wait_ge(qk_ps, 2 * g + 1)
                if g >= 2:
                    act.wait_ge(k_done, QH * (g - 1))
                act.activation(all_keys[:, g % 2], qk_bank(g, 1), ACT.Identity,
                               bias=sm[:, COL["bk"][0] + g:COL["bk"][0] + g + 1]).then_inc(all_keys_done, 1)
                act.wait_ge(qk_ps, 2 * g + 2)
                src = qk_bank(g, 0)
                for m in range(MEMBERS):
                    rows = slice(m * DB, (m + 1) * DB)
                    act.activation(queries[rows, g, :, m * SEQ:(m + 1) * SEQ], src[rows], ACT.Identity,
                                   bias=sm[rows, COL["bq"][0] + g:COL["bq"][0] + g + 1]).then_inc(q_done, 1)
            for p in range(PAIRS + 3):
                if p < PAIRS:
                    act.wait_ge(shift_done, p + 1)
                    if p >= 2:
                        act.wait_ge(probs_done, p - 1)
                    act.activation(expd[:, p % 2, :], shifted[:, p % 2, :], ACT.Exp, scale=ATT_SCALE)\
                        .then_inc(exp_done, 1)
                if 2 <= p < PAIRS + 2 and p != PAIRS:
                    q = p - 2
                    act.wait_ge(probs_ps, q + 1)
                    if q >= 2:
                        act.wait_ge(ctx_ps, q - 1)
                    act.activation(probs_t[:, q % 2].rearrange("k g q -> k (g q)"),
                                   bank[PROBS_BANK][0:KEYS, 0:VG * PAIR_TOKENS], ACT.Copy)\
                        .then_inc(probs_t_done, 1)
                if p >= 3 and p != PAIRS:
                    q = p - 3
                    act.wait_ge(ctx_ps, q + 1)
                    for c in range(2):
                        act.activation(ctx_t[:, c, q * PAIR_TOKENS:(q + 1) * PAIR_TOKENS],
                                       bank[CTX_BANK][:, c * PAIR_TOKENS:(c + 1) * PAIR_TOKENS], ACT.Identity,
                                       bias=sm[:, COL["bv"][0] + c:COL["bv"][0] + c + 1]).then_inc(ctx_done, 1)
                if p < PAIRS - 1:
                    split_hi_piece(p + 2)
                if p == PAIRS - 1:
                    deviations(0)
                if p == PAIRS:
                    deviations(1)
                    split_hi_piece(PIECES - 3)
                if p == PAIRS + 1:
                    h1_rounded(0)
                    deviations(2)
            split_hi_piece(PIECES - 2)
            deviations(3)
            split_hi_piece(PIECES - 1)
            deviations(4)
            shares(0)

            def hidden_hi(u):
                n = part_range(units[u][0])[1]
                r = u % RING
                act.wait_ge(hid_done, u + 1)
                if u >= RING:
                    act.wait_ge(down_ps, tiles_down(u - RING))
                act.activation(hid_hi[:, r, 0:n], hid[:, r, 0:n], ACT.Copy).then_inc(hid_hi_done, 1)

            for u in range(LAST_STEP):
                if u < UNITS:
                    part, t = units[u]
                    n = part_range(part)[1]
                    act.wait_ge(gate_done, u + 1)
                    if u >= RING:
                        act.wait_ge(sigw_done, u - RING + 1)
                    act.activation(sig[:, u % RING, 0:n], gate[:, u % GU_RING, 0:n], ACT.Sigmoid, scale=ALPHA)\
                        .then_inc(sig_done, 1)
                if u == 1:
                    route_rounded(0)
                if u == 12:
                    route_rounded(1)
                for v in due(u, SPREAD):
                    n = part_range(units[v][0])[1]
                    act.wait_ge(spread_ps, v + 1)
                    if v >= RING:
                        act.wait_ge(sigw_done, v - RING + 1)
                    act.activation(spread[:, v % RING, 0:n], bank[spread_bank(v)][:, 0:n], ACT.Copy)\
                        .then_inc(spread_done, 1)
                for v in due(u, HIDDEN):
                    if v == UNITS - 2:
                        act.wait_ge(mv2_done, 2)
                        act.activation(std[:, 0:2], mv[:, 0:2, 1], ACT.Sqrt, bias=eps[:]).then_inc(std2_done, 1)
                    hidden_hi(v)
                if u == 3:
                    h1_rounded(1)
                if u == 9:
                    shares(1)
            act.wait_ge(mv2_done, TILES)
            act.activation(std[:, 2:TILES], mv[:, 2:TILES, 1], ACT.Sqrt, bias=eps[:]).then_inc(std2_done, 1)
            i = TILES - 1
            act.wait_ge(shift2_done, 1)
            act.activation(result[0:LAST, i, :], acc(i), ACT.Identity, bias=shift2[0:LAST, :],
                           scale=rstd[0:LAST, i:i + 1]).then_inc(last_done, 1)

        @block.vector
        def _(dve):
            dve.memset(zeros_bf[:], 0.0).then_inc(zeros_done, 1)
            dve.memset(eps[:], EPS).then_inc(prep_done, 1)
            dve.memset(route_st[:].bitcast(F32), 0.0).then_inc(prep_done, 1)
            dve.memset(res_a[:, TOKENS:PADDED], 0.0).then_inc(prep_done, 1)
            dve.memset(res_b[:, TOKENS:PADDED], 0.0).then_inc(prep_done, 1)
            for e in range(EXPERTS):
                dve.memset(expert_ids[:, e:e + 1], float(e)).then_inc(prep_done, 1)
            dve.memset(wqk_lo[:].bitcast(F32), 0.0).then_inc(zero_fill, 1)

            for c in range(CHUNKS):
                dve.wait_ge(x_hi_done, c + 1)
                if c >= X_RING:
                    dve.wait_ge(emb_chunk, c - X_RING + 1)
                dve.tensor_tensor(x_lo[:, c % X_RING, :], x_raw[:, c, :], x_hi[:, c % X_RING, :].bitcast(F32),
                                  ALU.subtract).then_inc(x_lo_done, 1)
            dve.wait_ge(small_in, 16)
            for part, rows in (("a", P), ("b", DB)):
                pos, bias, cls = (col(f"{n}_{part}", rows) for n in ("pos", "bemb", "cls"))
                dve.tensor_scalar(pos[:, 1:SEQ], pos[:, 1:SEQ], bias, None, ALU.add).then_inc(prep_done, 1)
                dve.tensor_scalar(pos[:, 0:1], pos[:, 0:1], cls, None, ALU.add).then_inc(prep_done, 1)
            dve.wait_ge(prep_done, POSITIONS)
            def embedded(n):
                half, res, rows, part = n % 2, (res_a, res_b)[n // 2], (P, DB)[n // 2], "ab"[n // 2]
                dve.wait_ge(emb_done, n + 1)
                dve.tensor_tensor(
                    res[:, half * HALF:(half + 1) * HALF].rearrange("d (b k) -> d b k", k=SEQ),
                    bank[n][0:rows, 0:HALF].rearrange("d (b k) -> d b k", k=SEQ),
                    col(f"pos_{part}", rows).unsqueeze(1).broadcast_to([rows, IMAGES // 2, SEQ]),
                    ALU.add).then_inc(res_done if n < 2 else res_b_part, 1)
                if n >= 2:
                    dve.wait_ge(res_b_part, n - 1)
                    dve.tensor_tensor(res[:, half * HALF:(half + 1) * HALF],
                                      res[:, half * HALF:(half + 1) * HALF], bank[n][DB:P, 0:HALF], ALU.add)\
                        .then_inc(res_done, 1)

            def rests(n):
                half, res = n % 2, (res_a, res_b)[n // 2]
                hi, lo = ((h_ahi[:], h_alo[:]), (h_bst[0:DB, :], h_bst[DB:P, :]))[n // 2]
                dve.wait_ge(res_done, n + 1)
                dve.wait_ge(h_hi_done, n + 1)
                dve.tensor_tensor(slots(lo, half), by_pair(res[:, half * HALF:(half + 1) * HALF]),
                                  slots(hi.bitcast(F32), half), ALU.subtract).then_inc(h_lo_done, 1)

            for n in range(5):
                if n < 4:
                    embedded(n)
                if n >= 1:
                    rests(n - 1)
            dve.wait_ge(wv_hi_done, 1)
            dve.tensor_tensor(wv_lo[:], wv_raw[:], wv_hi[:].bitcast(F32), ALU.subtract)\
                .then_inc(wv_lo_done, 1)
            dve.memset(values[:, :, :, :, VH * HD:VW], 0.0).then_inc(zero_fill, 1)
            dve.tensor_copy(ident_bf[:], col("ident")).then_inc(prep_done, 1)
            dve.tensor_copy(causal_bf[:], col("causal")).then_inc(prep_done, 1)
            dve.tensor_scalar(bu1[:], col("bu"), 1.0, None, ALU.add).then_inc(prep_done, 1)
            wr = sm[:, COL["wr_a"][0]:COL["wr_b"][1]].rearrange("d (r e) -> d r e", r=2)
            dve.tensor_copy(wr_sb[:, :, 0], wr).then_inc(prep_done, 1)
            dve.tensor_copy(bd_hi[:], col("bd", 40)).then_inc(prep_done, 1)
            dve.wait_ge(prep_done, PREP)
            dve.tensor_tensor(wr_sb[:, :, 1], wr, wr_sb[:, :, 0].bitcast(F32), ALU.subtract).then_inc(prep_done, 1)
            dve.tensor_tensor(bd_lo[:], col("bd", 40), bd_hi[:].bitcast(F32), ALU.subtract)\
                .then_inc(prep_done, 1)

            for g in range(QG):
                dve.wait_ge(all_keys_done, g + 1)
                for h in range(QH):
                    keep = sm[:, COL["head_mask"][0] + h:COL["head_mask"][0] + h + 1]
                    dve.tensor_scalar(keys[:, g, :, h, :], all_keys[:, g % 2], keep, None, ALU.mult)\
                        .then_inc(k_done, 1)

            def value_rows(p):
                dve.wait_ge(v_ps, p + 1)
                if p == 0:
                    dve.wait_ge(zero_fill, 2)
                src = bank[VALUES_BANK[p % 2]][0:KEYS, 0:MEMBERS * D].rearrange("k (s c) -> k s c", c=VH * HD)
                keep = col("value_mask", KEYS).unsqueeze(1).broadcast_to([KEYS, MEMBERS * VG, VH * HD])
                dst = values[:, :, p, :, 0:VH * HD]
                dve.tensor_tensor(dst, src.rearrange("k (m g) c -> k m g c", m=MEMBERS),
                                  keep.rearrange("k (m g) c -> k m g c", m=MEMBERS), ALU.mult)\
                    .then_inc(v_done, 1)

            def by_head(t):
                return t.rearrange("q (h k) -> q h k", h=HEADS)

            def pair_step(p):
                if p < PAIRS:
                    src = by_head(bank[SCORES_BANK[p % 2]][0:PAIR_TOKENS, 0:SCORES])
                    dve.wait_ge(scores_ps, p + 1)
                    dve.tensor_reduce(top_score[:, p % 2, :], src, AX_X, ALU.max).then_inc(top_done, 1)
                if p >= 1:
                    q = p - 1
                    dve.wait_ge(exp_done, q + 1)
                    dve.tensor_reduce(prob_sum[:, q % 2, :], by_head(expd[:, q % 2, :]), AX_X, ALU.add)\
                        .then_inc(sum_done, 1)
                if p < PAIRS:
                    dve.wait_ge(top_done, p + 1)
                    if p >= 2:
                        dve.wait_ge(exp_done, p - 1)
                    dve.tensor_tensor(by_head(shifted[:, p % 2, :]), src,
                                      top_score[:, p % 2, :].unsqueeze(2).broadcast_to([PAIR_TOKENS, HEADS, SEQ]),
                                      ALU.subtract).then_inc(shift_done, 1)
                if p >= 1:
                    dve.wait_ge(sum_done, q + 1)
                    if q >= 2:
                        dve.wait_ge(probs_done, q - 1)
                    dve.reciprocal(prob_inv[:, q % 2, :], prob_sum[:, q % 2, :]).then_inc(inv_done, 1)

            def norm_stats(i):
                dve.wait_ge(y_ps, i + 1)
                dve.bn_stats(stats[:, i, :], bank[Y_BANK[i]][:, 0:D]).then_inc(stats_done, 1)
                dve.wait_ge(stats_done, i + 1)
                dve.bn_aggr(mv[:, i, :], stats[:, i, :]).then_inc(mv_done, 1)

            def norm_apply(i):
                dve.wait_ge(std_done, i + 1)
                dve.reciprocal(rstd[:, i:i + 1], std[:, i:i + 1]).then_inc(rstd_done, 1)
                dve.wait_ge(rstd_done, i + 1)
                dve.wait_ge(mv_done, i + 1)
                dve.tensor_scalar(h1[:, i, :], bank[Y_BANK[i]][:, 0:D], mv[:, i, 0:1], rstd[:, i:i + 1],
                                  ALU.subtract, ALU.mult).then_inc(h1_done, 1)

            def h1_rests(part):
                c0 = PARTS[part][0] * P
                n = (PARTS[part][1] - PARTS[part][0]) * P
                bank_a, bank_b = H1T_BANK[part]
                dve.wait_ge(h1_hi_done, 2 * part + 1)
                dve.tensor_tensor(h1_alo[:, c0:c0 + n], bank[bank_a][:, 0:n],
                                  h1_ahi[:, c0:c0 + n].bitcast(F32), ALU.subtract).then_inc(h1_lo_done, 1)
                dve.wait_ge(h1_hi_done, 2 * part + 2)
                dve.tensor_tensor(h1_bst[DB:P, c0:c0 + n], bank[bank_b][0:DB, 0:n],
                                  h1_bst[0:DB, c0:c0 + n].bitcast(F32), ALU.subtract).then_inc(h1_lo_done, 1)

            for p in range(PAIRS + 1):
                if p == 0:
                    value_rows(0)
                pair_step(p)
                if 1 <= p < PAIRS:
                    value_rows(p)
                if p == 6:
                    norm_stats(0)
            q = PAIRS - 2
            dve.wait_ge(probs_ps, q + 1)
            dve.wait_ge(probs_t_done, q)
            dve.wait_ge(ctx_ps, q - 1)
            dve.tensor_copy(probs_t[:, q % 2].rearrange("k g q -> k (g q)"),
                            bank[PROBS_BANK][0:KEYS, 0:VG * PAIR_TOKENS]).then_inc(probs_t_done, 1)
            q = PAIRS - 3
            dve.wait_ge(ctx_ps, q + 1)
            dve.tensor_tensor(ctx_t[:, :, q * PAIR_TOKENS:(q + 1) * PAIR_TOKENS],
                              bank[CTX_BANK][:, 0:2 * PAIR_TOKENS].rearrange("d (c q) -> d c q", c=2),
                              col("bv").unsqueeze(2).broadcast_to([P, 2, PAIR_TOKENS]), ALU.add)\
                .then_inc(ctx_done, 2)
            norm_stats(1)
            norm_apply(0)
            norm_apply(1)

            def choose(part, steps=range(5)):
                a, b = PARTS[part]
                n = b - a
                for step in steps:
                    if step == 0:
                        dve.wait_ge(logit_ps, part + 1)
                        both = bank[ROUTER_BANK[part]][:, 0:2 * n * EXPERTS]\
                            .rearrange("t (i s e) -> t i s e", s=2, e=EXPERTS)
                        dve.tensor_tensor(logits[:, a:b, :], both[:, :, 0],
                                          col("br").unsqueeze(1).broadcast_to([P, n, EXPERTS]), ALU.add)\
                            .then_inc(router, 1)
                        dve.wait_ge(router, 6 * part + 1)
                        dve.tensor_tensor(logits[:, a:b, :], logits[:, a:b, :], both[:, :, 1], ALU.add)\
                            .then_inc(router, 1)
                    if step == 1:
                        dve.wait_ge(router, 6 * part + 2)
                        for i in range(a, b):
                            ins = dve.max(top[:, i, :], logits[:, i, :])
                        ins.then_inc(router, 1)
                    if step == 2:
                        dve.wait_ge(router, 6 * part + 3)
                        for i in range(a, b):
                            ins = dve.max_index(top_id[:, i, :], top[:, i, :], logits[:, i, :])
                        ins.then_inc(router, 1)
                        dve.tensor_tensor(gap[:, a:b], top[:, a:b, 0], top[:, a:b, 1], ALU.subtract)\
                            .then_inc(router, 1)
                    if step == 3:
                        dve.wait_ge(router, 6 * part + 5)
                        dve.tensor_copy(top_idf[:, a:b, :], top_id[:, a:b, 0:2]).then_inc(router, 1)
                    if step == 4:
                        dve.wait_ge(router, 6 * part + 6)
                        for k in range(2):
                            ins = dve.tensor_tensor(
                                pick[:, k, a:b, :], expert_ids[:].unsqueeze(1).broadcast_to([P, n, EXPERTS]),
                                top_idf[:, a:b, k:k + 1].broadcast_to([P, n, EXPERTS]), ALU.is_equal)
                        ins.then_inc(route_done, 1)

            def share_out(part):
                a, b = PARTS[part]
                n = b - a
                dve.wait_ge(route_done, 3 * part + 1)
                dve.wait_ge(share_done, 2 * part + 2)
                for k in range(2):
                    ins = dve.tensor_tensor(pick[:, k, a:b, :], pick[:, k, a:b, :],
                                            share[:, k, a:b].unsqueeze(2).broadcast_to([P, n, EXPERTS]),
                                            ALU.mult)
                ins.then_inc(route_done, 1)
                dve.wait_ge(route_done, 3 * part + 2)
                dve.tensor_tensor(route[:, a:b, :], pick[:, 0, a:b, :], pick[:, 1, a:b, :], ALU.add)\
                    .then_inc(route_done, 1)

            def route_rests(part):
                a, b = PARTS[part]
                dve.wait_ge(route_hi_done, part + 1)
                dve.tensor_tensor(route_st[32:40, a * P:b * P], bank[ROUTER_BANK[part]][0:EXPERTS, 0:(b - a) * P],
                                  route_st[0:EXPERTS, a * P:b * P].bitcast(F32), ALU.subtract)\
                    .then_inc(route_lo_done, 1)

            def gates(u):
                part, t = units[u]
                n = part_range(part)[1]
                r = u % GU_RING
                dve.wait_ge(gate_ps, u + 1)
                if u >= GU_RING:
                    dve.wait_ge(glu_done, u - GU_RING + 1)
                dve.tensor_scalar(gate[:, r, 0:n], bank[GATE_BANK[u % 2]][:, 0:n],
                                  sm[:, COL["bg"][0] + t:COL["bg"][0] + t + 1], LIMIT, ALU.add, ALU.min)\
                    .then_inc(gate_done, 1)
                dve.wait_ge(up_ps, u + 1)
                if u >= GU_RING:
                    dve.wait_ge(hid_done, u - GU_RING + 1)
                dve.tensor_scalar(up[:, r, 0:n], bank[UP_BANK[u % 2]][:, 0:n], bu1[:, t:t + 1], LIMIT + 1.0,
                                  ALU.add, ALU.min).then_inc(up_done, 1)

            def hidden(u):
                n = part_range(units[u][0])[1]
                r = u % RING
                if u >= UNITS - GLU_ON_DVE:
                    dve.wait_ge(sigw_done, u + 1)
                    dve.wait_ge(hid_done, u - RING + 1)
                    dve.tensor_tensor(glu[:, r, 0:n], sig_w[:, r, 0:n], gate[:, u % GU_RING, 0:n], ALU.mult)\
                        .then_inc(glu_done, 1)
                dve.wait_ge(glu_done, u + 1)
                dve.wait_ge(up_done, u + 1)
                if u >= RING:
                    dve.wait_ge(hid_hi_done, u - RING + 1)
                    dve.wait_ge(hid_lo_done, u - RING + 1)
                dve.scalar_tensor_tensor(out=hid[:, r, 0:n], in0=up[:, u % GU_RING, 0:n], scalar=1.0 - LIMIT,
                                         in1=glu[:, r, 0:n], op0=ALU.max, op1=ALU.mult).then_inc(hid_done, 1)

            def hidden_lo(u):
                n = part_range(units[u][0])[1]
                r = u % RING
                dve.wait_ge(hid_hi_done, u + 1)
                if u >= RING:
                    dve.wait_ge(down_ps, tiles_down(u - RING))
                dve.tensor_tensor(hid_lo[:, r, 0:n], hid[:, r, 0:n], hid_hi[:, r, 0:n].bitcast(F32),
                                  ALU.subtract).then_inc(hid_lo_done, 1)

            def sum_h1(i):
                dve.wait_ge(down_ps, tiles_down(FT - 1))
                dve.tensor_tensor(y2[:, i, :], acc(i), h1[:, i, :], ALU.add).then_inc(y2_done, 1)

            def before_norm(i):
                return y2[:, i, :] if i < 2 else acc(i)

            def sum_stats(*tiles):
                for i in tiles:
                    rows = LAST if i == TILES - 1 else P
                    if i < 2:
                        dve.wait_ge(y2_done, i + 1)
                    else:
                        dve.wait_ge(down_ps, tiles_down(UNITS - 1) - (TILES - 1 - i))
                    dve.bn_stats(stats[0:rows, i, :], before_norm(i)).then_inc(stats2_done, 1)
                for n, i in enumerate(tiles):
                    rows = LAST if i == TILES - 1 else P
                    dve.wait_ge(stats2_done, tiles[0] + n + 1)
                    dve.bn_aggr(mv[0:rows, i, :], stats[0:rows, i, :]).then_inc(mv2_done, 1)

            def results(lot, tiles):
                a, b = PARTS[lot]
                dve.wait_ge(std2_done, lot + 1)
                dve.reciprocal(rstd[:, a:b], std[:, a:b]).then_inc(rstd2_done, 1)
                dve.wait_ge(rstd2_done, lot + 1)
                if lot == 1:
                    i = TILES - 1
                    dve.scalar_tensor_tensor(out=shift2[0:LAST, :], in0=mv[0:LAST, i, 0:1], scalar=-1.0,
                                             in1=rstd[0:LAST, i:i + 1], op0=ALU.mult, op1=ALU.mult)\
                        .then_inc(shift2_done, 1)
                for i in tiles:
                    rows = LAST if i == TILES - 1 else P
                    dve.tensor_scalar(result[0:rows, i, :], before_norm(i), mv[0:rows, i, 0:1],
                                      rstd[0:rows, i:i + 1], ALU.subtract, ALU.mult).then_inc(result_done, 1)

            norm_stats(2)
            h1_rests(0)
            norm_apply(2)
            norm_stats(3)
            choose(0, [0])
            norm_apply(3)
            choose(0, [1])
            norm_stats(4)
            choose(0, [2])
            norm_apply(4)
            choose(0, [3, 4])
            for u in range(LAST_STEP):
                if u < UNITS:
                    gates(u)
                if u == 0:
                    share_out(0)
                if u == 1:
                    route_rests(0)
                if u == 4:
                    h1_rests(1)
                if u in (8, 9, 10):
                    choose(1, [(0, 2, 4)[u - 8]])
                for v in due(u, HIDDEN):
                    hidden(v)
                for v in due(u, LO):
                    hidden_lo(v)
                if u in (8, 9):
                    choose(1, [(1, 3)[u - 8]])
                if u == 10:
                    share_out(1)
                if u == 12:
                    route_rests(1)
                if u == FIRST_PART_DOWN:
                    sum_h1(0)
                    sum_h1(1)
                if u == FIRST_PART_DOWN + 2:
                    sum_stats(0, 1)
            results(0, (0, 1))
            sum_stats(2, 3, 4)
            dve.wait_ge(mv2_done, TILES)
            results(1, (2, 3))

        @block.tensor
        def _(pe):
            pe.wait_ge(zeros_done, 1)
            for _ in range(WARM_UP):
                pe.matmul(bank[7][:, :], zeros_bf[:, 0:P], zeros_bf[:], start=True, stop=True)
            a_hi, a_lo, b_both = slice(0, P), slice(2 * P, 3 * P), slice(P, 2 * P)
            HI_TERMS = ((0, a_hi), (1, a_hi), (2, b_both), (3, b_both), (0, a_lo), (1, a_lo))
            LO_TERMS = ((0, a_hi), (1, a_hi), (2, b_both), (3, b_both))

            def embed(b, w, x, c, start, stop):
                half = b % 2
                return pe.matmul(bank[b][:, 0:HALF], we_sb[:, c, w],
                                 x[:, c % X_RING, half * HALF:(half + 1) * HALF], start=start, stop=stop)

            for c in range(CHUNKS - 2):
                pe.wait_ge(we_lo_done, 2 * (c + 1))
                pe.wait_ge(x_hi_done, c + 1)
                for b, w in HI_TERMS:
                    embed(b, w, x_hi, c, c == 0 and w is not a_lo, False)
                pe.wait_ge(x_lo_done, c + 1)
                for b, w in LO_TERMS:
                    mm = embed(b, w, x_lo, c, False, False)
                mm.then_inc(emb_chunk, 1)
            pe.wait_ge(we_lo_done, 2 * CHUNKS)
            pe.wait_ge(x_hi_done, CHUNKS)
            pe.wait_ge(x_lo_done, CHUNKS)
            for out_bank in range(4):
                for c in (CHUNKS - 2, CHUNKS - 1):
                    for terms, x in ((HI_TERMS, x_hi), (LO_TERMS, x_lo)):
                        for b, w in terms:
                            if b == out_bank:
                                mm = embed(b, w, x, c, False, c == CHUNKS - 1 and x is x_lo)
                mm.then_inc(emb_done, 1)

            A_HI, A_LO, B_ALL = ((wqk_hi, 0, h_ahi), (wqk_lo, 0, h_ahi)), ((wqk_hi, 0, h_alo),), \
                ((wqk_hi, 1, h_bst), (wqk_lo, 1, h_bst))

            def query_keys(n, terms):
                g, w = n // 2, 1 - n % 2
                for m in range(MEMBERS):
                    wc = slice(DB - m * DB, DB - m * DB + P)
                    hc = slice(m * HALF, (m + 1) * HALF)
                    for wt, r, h in terms:
                        mm = pe.matmul(bank[QK_BANK[n]][:, 0:HALF], wt[:, w, r, g, wc], h[:, hc],
                                       start=(h is h_ahi and m == 0 and wt is wqk_hi),
                                       stop=(h is h_bst and m == 1 and wt is wqk_lo))
                if h is h_bst:
                    mm.then_inc(qk_ps, 1)

            EARLY = 4
            pe.wait_ge(wqk_lo_done, 2)
            pe.wait_ge(h_hi_done, 2)
            for n in range(EARLY):
                query_keys(n, A_HI)
            pe.wait_ge(h_lo_done, 2)
            for n in range(EARLY):
                query_keys(n, A_LO)
            pe.wait_ge(wqk_lo_done, 4)
            pe.wait_ge(h_hi_done, 4)
            pe.wait_ge(h_lo_done, 4)
            for n in range(2 * QG):
                if n < EARLY:
                    query_keys(n, B_ALL)
                else:
                    query_keys(n, A_HI + A_LO + B_ALL)

            def scores(p):
                ps = bank[SCORES_BANK[p % 2]]
                if p == 0:
                    pe.wait_ge(prep_done, PREP + 2)
                    pe.wait_ge(q_done, 2 * QG)
                    pe.wait_ge(k_done, QG * QH)
                if p >= 2:
                    pe.wait_ge(shift_done, p - 1)
                pe.matmul(ps[0:PAIR_TOKENS, 0:SCORES].rearrange("q (h k) -> q h k", h=HEADS),
                          ident_bf[0:PAIR_TOKENS, 0:PAIR_TOKENS],
                          causal_bf[0:PAIR_TOKENS, :].unsqueeze(1).broadcast_to([PAIR_TOKENS, HEADS, SEQ]),
                          start=True, stop=False)
                for g in range(QG):
                    mm = pe.matmul(ps[0:PAIR_TOKENS, g * QH * SEQ:(g + 1) * QH * SEQ], queries[:, g, p, :],
                                   keys[:, g, p].rearrange("d h k -> d (h k)"), start=False, stop=(g == QG - 1))
                mm.then_inc(scores_ps, 1)

            def pair_values(p):
                if p == 0:
                    pe.wait_ge(rep_done, 3)
                    pe.wait_ge(wv_lo_done, 1)
                    pe.wait_ge(q_done, 2 * QG - 2)
                if p >= 2:
                    pe.wait_ge(v_done, p - 1)
                for m in range(MEMBERS):
                    terms = ((rep[0], wv_hi, 0), (rep[0], wv_lo, 0), (rep[1], wv_hi, 0),
                             (rep[2], wv_hi, 1), (rep[2], wv_lo, 1))
                    for k, (h, wt, r) in enumerate(terms):
                        mm = pe.matmul(bank[VALUES_BANK[p % 2]][0:KEYS, m * D:(m + 1) * D],
                                       h[:, m * PAIRS + p].rearrange("d v k -> d (v k)"), wt[:, r, :],
                                       start=(k == 0), stop=(k == 4))
                mm.then_inc(v_ps, 1)

            def turn(p):
                pe.wait_ge(probs_done, p + 1)
                if p >= 1:
                    pe.wait_ge(probs_t_done, p)
                for g in range(VG):
                    mm = pe.transpose(bank[PROBS_BANK][0:KEYS, g * PAIR_TOKENS:(g + 1) * PAIR_TOKENS],
                                      probs[:, p % 2, g * KEYS:(g + 1) * KEYS],
                                      sm[0:PAIR_TOKENS, COL["ident"][0]:COL["ident"][0] + PAIR_TOKENS])
                mm.then_inc(probs_ps, 1)

            def contexts(p):
                pe.wait_ge(probs_t_done, p + 1)
                pe.wait_ge(v_done, p + 1)
                if p >= 1:
                    pe.wait_ge(ctx_done, 2 * p)
                for m in range(MEMBERS):
                    for g in range(VG):
                        r0, c0 = VW * (g % 2), (g // 2) * PAIR_TOKENS + m * SEQ
                        mm = pe.matmul(bank[CTX_BANK][r0:r0 + VW, c0:c0 + SEQ], values[:, m, p, g, :],
                                       probs_t[:, p % 2, g, m * SEQ:(m + 1) * SEQ], start=True, stop=True)
                mm.then_inc(ctx_ps, 1)

            ident = col("ident")

            def project(i):
                cols = slice(i * P, (i + 1) * P)
                y = bank[Y_BANK[i]]
                pe.matmul(y[:, 0:D], ctx_t[:, 0, cols], wo_sb[:, 0, :], start=True, stop=False)
                pe.matmul(y[:, 0:D], ctx_t[:, 1, cols], wo_sb[:, 1, :], start=False, stop=False)
                pe.matmul(y[:, 0:P], res_a[:, cols], ident, start=False, stop=False)
                pe.matmul(y[:, P:D], res_b[:, cols], ident[0:DB, 0:DB], start=False, stop=True)\
                    .then_inc(y_ps, 1)

            def turn_h1(part):
                a, b = PARTS[part]
                pe.wait_ge(h1_done, b)
                for r, (c0, c1) in enumerate(((0, P), (P, D))):
                    for i in range(a, b):
                        mm = pe.transpose(bank[H1T_BANK[part][r]][0:c1 - c0, (i - a) * P:(i - a + 1) * P],
                                          h1[:, i, c0:c1], ident)
                    mm.then_inc(h1t_ps, 1)

            def router_logits(part, tiles):
                a, b = PARTS[part]
                pe.wait_ge(h1_hi_done, 2 * part + 2)
                pe.wait_ge(h1_lo_done, 2 * part + 2)
                if part == 0:
                    pe.wait_ge(v_done, PAIRS)
                for i in tiles:
                    cols = slice(i * P, (i + 1) * P)
                    for k, (h, r) in enumerate(((h1_ahi, 0), (h1_alo, 0), (h1_bst, 1))):
                        mm = pe.matmul(bank[ROUTER_BANK[part]][:, (i - a) * 2 * EXPERTS:(i - a + 1) * 2 * EXPERTS],
                                       h[:, cols], wr_sb[:, r].rearrange("d s e -> d (s e)"),
                                       start=(k == 0), stop=(k == 2))
                if tiles[-1] == b - 1:
                    mm.then_inc(logit_ps, 1)

            def gate_up(u):
                part, t = units[u]
                t0, n = part_range(part)
                lot = t // TL
                if t == 0:
                    pe.wait_ge(h1_lo_done, 2 * part + 2)
                if part == 0 and t % TL == 0:
                    pe.wait_ge(split_done, 2 * lot + 2)
                for which, done, used in ((0, gate_ps, gate_done), (1, up_ps, up_done)):
                    if u >= 2:
                        pe.wait_ge(used, u - 1)
                    ps = bank[(GATE_BANK, UP_BANK)[which][u % 2]][:, 0:n]
                    wa, wb = expert_weights(t, which)
                    terms = ((experts_hi, wa, h1_ahi), (experts_lo, wa, h1_ahi), (experts_hi, wa, h1_alo),
                             (experts_hi, wb, h1_bst), (experts_lo, wb, h1_bst))
                    for k, (wt, w, h) in enumerate(terms):
                        mm = pe.matmul(ps, wt[:, lot, w], h[:, t0:t0 + n], start=(k == 0), stop=(k == 4))
                    mm.then_inc(done, 1)

            def routes(part):
                a, b = PARTS[part]
                pe.wait_ge(route_done, 3 * part + 3)
                for i in range(a, b):
                    mm = pe.transpose(bank[ROUTER_BANK[part]][0:EXPERTS, (i - a) * P:(i - a + 1) * P],
                                      route[:, i, :], ident)
                mm.then_inc(route_ps, 1)

            def spreads(u):
                part, t = units[u]
                t0, n = part_range(part)
                if t == 0:
                    pe.wait_ge(route_lo_done, part + 1)
                if u == 3:
                    pe.wait_ge(h1_lo_done, 4)
                before = [v for v in range(u) if spread_bank(v) == spread_bank(u)]
                if before:
                    pe.wait_ge(spread_done, before[-1] + 1)
                pe.matmul(bank[spread_bank(u)][:, 0:n], sel_sb[:, t * P:(t + 1) * P], route_st[:, t0:t0 + n],
                          start=True, stop=True).then_inc(spread_ps, 1)

            def down(u):
                part, t = units[u]
                a, b = PARTS[part]
                pe.wait_ge(hid_lo_done, u + 1)
                for i in range(a, b):
                    rows = LAST if i == TILES - 1 else P
                    cols = slice((i - a) * P, (i - a) * P + rows)
                    if t == 0:
                        if i == TILES - 1:
                            pe.wait_ge(y2_done, 2)
                        for k, wt in enumerate((bd_hi, bd_lo)):
                            pe.matmul(acc(i), route_st[:, i * P:i * P + rows], wt[:],
                                      start=(k == 0 and i != 1), stop=False, skip_group_check=True)
                    for k, (h, wt) in enumerate(((hid_hi, experts_hi), (hid_lo, experts_hi),
                                                 (hid_hi, experts_lo))):
                        mm = pe.matmul(acc(i), h[:, u % RING, cols], wt[:, t // TL, down_weights(t)],
                                       start=False, stop=(t == FT - 1 and k == 2), skip_group_check=True)
                    mm.then_inc(down_ps, 1)

            pair_values(0)
            for p in range(PAIRS + 3):
                if p < PAIRS:
                    scores(p)
                if 1 <= p < PAIRS:
                    pair_values(p)
                if 2 <= p < PAIRS + 2:
                    turn(p - 2)
                if p == PAIRS + 2:
                    pe.wait_ge(ctx_done, 2 * 6)
                    pe.wait_ge(shift_done, PAIRS)
                    project(2)
                    turn_h1(0)
                if p >= 3:
                    contexts(p - 3)
                if p == 5:
                    pe.wait_ge(wo_in, 16)
                    pe.wait_ge(ctx_done, 2 * 2)
                    project(0)
                if p == 7:
                    pe.wait_ge(ctx_done, 2 * 4)
                    project(1)
            pe.wait_ge(ctx_done, 2 * 7)
            project(3)
            router_logits(0, (0, 1))
            pe.wait_ge(ctx_done, 2 * PAIRS)
            project(4)
            pe.wait_ge(sel_done, 1)
            for u in range(LAST_STEP):
                if u < UNITS:
                    gate_up(u)
                if u == UNITS:
                    for i in range(*PARTS[1]):
                        rows = LAST if i == TILES - 1 else P
                        pe.matmul(acc(i), ident[:, 0:rows], h1[:, i, :], start=False, stop=False,
                                  skip_group_check=True)
                if u == 1:
                    turn_h1(1)
                    routes(0)
                for v in due(u, SPREAD)[:1]:
                    spreads(v)
                if u in (5, 6, 7):
                    router_logits(1, (u - 3,))
                for v in due(u, DOWN):
                    down(v)
                for v in due(u, SPREAD)[1:]:
                    spreads(v)
                if u == 11:
                    routes(1)


def kernel(**inputs):
    import numpy as np
    import concourse.bacc as bacc
    from concourse.bass_utils import run_bass_kernel_spmd

    x = np.asarray(inputs["x"])
    f = {k: np.asarray(v) for k, v in inputs.items()}
    side = 6
    px = 16

    patches = x.reshape(IMAGES, 3, side, px, side, px).transpose(0, 2, 4, 1, 3, 5)
    patches = patches.reshape(IMAGES, SEQ - 1, PATCH_DIM)
    patches = np.pad(patches, ((0, 0), (1, 0), (0, 0))).reshape(TOKENS, PATCH_DIM)
    x_t = patches.T.reshape(CHUNKS, P, TOKENS).transpose(1, 0, 2)
    w_emb = f["L0_tok_W_emb"].reshape(CHUNKS, P, D).transpose(1, 0, 2)

    def a_b(w):
        return np.stack([w[:P], np.concatenate([w[P:], w[P:]])], axis=1)

    def flat(w):
        return w.transpose(1, 0, 2).reshape(D, HEADS * HD)

    w_qk = np.stack([a_b(flat(f["L0_attn_Wq"])), a_b(flat(f["L0_attn_Wk"]))], axis=1)
    w_v = a_b(flat(f["L0_attn_Wv"]))
    wo = np.zeros((P, 2, D), np.float32)
    bv = np.zeros((P, 2), np.float32)
    bv_flat = f["L0_attn_bv"].reshape(-1)
    used = VH * HD
    for g in range(VG):
        r0 = VW * (g % 2)
        wo[r0:r0 + used, g // 2] = f["L0_attn_Wo"][g * used:(g + 1) * used]
        bv[r0:r0 + used, g // 2] = bv_flat[g * used:(g + 1) * used]
    wo[used, 0] = f["L0_attn_bo"]
    bv[used, 0] = 1.0

    small = np.zeros((P, SMALL), np.float32)

    def put(name, a):
        c0, c1 = COL[name]
        small[:a.shape[0], c0:c1] = a.reshape(a.shape[0], -1)

    pos = f["L0_tok_pos_embedding"][0, :SEQ].T
    for part, rows in (("a", slice(0, P)), ("b", slice(P, D))):
        put(f"pos_{part}", pos[rows])
        put(f"bemb_{part}", f["L0_tok_b_emb"][rows][:, None])
        put(f"cls_{part}", f["L0_tok_cls_token"].reshape(-1)[rows][:, None])
    for name, b in (("bq", f["L0_attn_bq"]), ("bk", f["L0_attn_bk"])):
        t = b.reshape(QG, QH * HD).T
        put(name, np.concatenate([t, t]))
    put("bv", bv)
    put("bg", f["L0_ffn_bgu"][:, :INNER].reshape(FT, P).T)
    put("bu", f["L0_ffn_bgu"][:, INNER:].reshape(FT, P).T)
    put("br", np.broadcast_to(f["L0_ffn_br"], (P, EXPERTS)))
    wr = a_b(f["L0_ffn_Wr"])
    put("wr_a", wr[:, 0])
    put("wr_b", wr[:, 1])
    rows = np.arange(P)
    put("head_mask", (rows[:, None] % DB // HD == np.arange(QH)).astype(np.float32))
    keys = np.arange(KEYS)
    put("value_mask", (keys[:, None] // SEQ == np.arange(VH * HD) // HD).astype(np.float32))
    queries = np.arange(PAIR_TOKENS) % SEQ
    put("causal", np.where(np.arange(SEQ) > queries[:, None], MASKED, 0.0).astype(np.float32))
    put("ident", np.eye(P, dtype=np.float32))
    bd = np.zeros((40, D), np.float32)
    bd[0:EXPERTS] = f["L0_ffn_bd"]
    bd[32:40] = f["L0_ffn_bd"]
    put("bd", bd)

    owner = np.arange(EXPERTS * INNER) // INNER
    sel = np.zeros((40, FT * P), np.float32)
    sel[owner, np.arange(FT * P)] = 1.0
    sel[32 + owner, np.arange(FT * P)] = 1.0

    wgu = f["L0_ffn_Wgu"].transpose(1, 0, 2)
    g_ab = a_b(wgu[:, :, :INNER].reshape(D, FT * P))
    u_ab = a_b(wgu[:, :, INNER:].reshape(D, FT * P))
    w_d = f["L0_ffn_Wd"].reshape(FT, P, D).transpose(1, 0, 2)

    def lots(w):
        return w.reshape(P, LOTS, -1)

    w_experts = np.concatenate([lots(g_ab[:, 0]), lots(u_ab[:, 0]), lots(g_ab[:, 1]), lots(u_ab[:, 1]),
                                lots(w_d)], axis=2)

    nc = bacc.Bacc("TRN2", target_bir_lowering=False, num_devices=1)
    arrays, args = {}, []
    for name, a in (("x_t", x_t), ("w_emb", w_emb), ("small", small), ("w_qk", w_qk), ("w_v", w_v),
                    ("w_o", wo), ("sel", sel), ("w_experts", w_experts)):
        arrays[name] = np.ascontiguousarray(a)
        args.append(nc.dram_tensor(name, a.shape, mybir.dt.from_np(a.dtype), kind="ExternalInput").ap())
    args.append(nc.dram_tensor("out_0", (TOKENS, D), F32, kind="ExternalOutput").ap())
    build_program(nc, *args)
    r = run_bass_kernel_spmd(nc, [arrays], core_ids=[0])
    return r.results[0]["out_0"].reshape(IMAGES, SEQ, D)
```
